# Optimizing a Trainium2 kernel written in Bass

```python
import numpy as np
import jax
import jax.numpy as jnp

def _softmax(x, axis=-1):
    return jax.nn.softmax(x, axis=axis)

def _gelu(x):
    return jax.nn.gelu(x, approximate=True)

def _silu(x):
    return jax.nn.silu(x)

def _sigmoid(x):
    return jax.nn.sigmoid(x)

def _layernorm(x, axis=-1, eps=1e-05):
    m = jnp.mean(x, axis=axis, keepdims=True)
    v = jnp.var(x, axis=axis, keepdims=True)
    return (x - m) / jnp.sqrt(v + eps)

def _scatter_add(tgt, idx, src, axis=0):
    return tgt.at[idx].add(src)

def _segment_sum(src, seg, n):
    return jax.ops.segment_sum(src, seg, n)
kernel_name = 'mk_adj_resnorm_d2_adj_r2_5184ae'

def setup_inputs(seed: int=0):
    np.random.seed(seed)
    _w = jnp.asarray

    def _rec_inputs():
        import jax
        import jax.numpy as jnp
        _gk = jax.random.key(seed)
        x = -0.0002928 + 1 * jax.random.normal(jax.random.fold_in(_gk, 1), (4096, 256), jnp.float32)
        _a = jax.random.bernoulli(jax.random.fold_in(_gk, 2), 0.000976562, (4096, 4096))
        adj = _a.astype(jnp.int32)
        return (x, adj)
    x, adj = _rec_inputs()

    def _L0_gnn_setup():
        import jax, jax.numpy as jnp
        import numpy as np
        N = 4096
        D_IN = 256
        D_OUT = 256
        key = jax.random.key(seed)
        k1, k2, k3, k4 = jax.random.split(key, 4)
        node_feats = jax.random.normal(k1, (N, D_IN), dtype=jnp.float32)
        adj_matrix = jax.random.randint(k2, (N, N), 0, 2, dtype=jnp.int32)
        w_self = jax.random.normal(k3, (D_OUT, D_IN), dtype=jnp.float32) * D_IN ** (-0.5)
        w_neigh = jax.random.normal(k4, (D_OUT, D_IN), dtype=jnp.float32) * D_IN ** (-0.5)
        return {'node_feats': node_feats, 'adj_matrix': adj_matrix, 'w_self': w_self, 'w_neigh': w_neigh}
    _L0_gnn_all = _L0_gnn_setup()
    _L0_gnn_in = {k: v for k, v in _L0_gnn_all.items() if k in ('w_self', 'w_neigh')}
    del _L0_gnn_all

    def _L1_gnn_setup():
        import jax, jax.numpy as jnp
        import numpy as np
        N, D_IN, D_OUT = (4096, 256, 256)
        key = jax.random.key(seed)
        ks = jax.random.split(key, 8)
        scale_in = 1.0 / np.sqrt(D_IN)
        scale_cat = 1.0 / np.sqrt(2 * D_OUT)
        return {'x': jax.random.normal(ks[0], (N, D_IN), dtype=jnp.float32), 'adj': jax.random.randint(ks[1], (N, N), 0, 2, dtype=jnp.int32), 'W_self': jax.random.uniform(ks[2], (D_IN, D_OUT), jnp.float32, -scale_in, scale_in), 'b_self': jax.random.uniform(ks[3], (D_OUT,), jnp.float32, -scale_in, scale_in), 'W_nb': jax.random.uniform(ks[4], (D_IN, D_OUT), jnp.float32, -scale_in, scale_in), 'b_nb': jax.random.uniform(ks[5], (D_OUT,), jnp.float32, -scale_in, scale_in), 'W_comb': jax.random.uniform(ks[6], (2 * D_OUT, D_OUT), jnp.float32, -scale_cat, scale_cat), 'b_comb': jax.random.uniform(ks[7], (D_OUT,), jnp.float32, -scale_cat, scale_cat)}
    _L1_gnn_all = _L1_gnn_setup()
    _L1_gnn_in = {k: v for k, v in _L1_gnn_all.items() if k in ('W_self', 'b_self', 'W_nb', 'b_nb', 'W_comb', 'b_comb')}
    del _L1_gnn_all
    return {'x': x, 'adj': adj, 'L0_gnn_w_self': _L0_gnn_in['w_self'], 'L0_gnn_w_neigh': _L0_gnn_in['w_neigh'], 'L1_gnn_W_self': _L1_gnn_in['W_self'], 'L1_gnn_b_self': _L1_gnn_in['b_self'], 'L1_gnn_W_nb': _L1_gnn_in['W_nb'], 'L1_gnn_b_nb': _L1_gnn_in['b_nb'], 'L1_gnn_W_comb': _L1_gnn_in['W_comb'], 'L1_gnn_b_comb': _L1_gnn_in['b_comb']}

def reference(x, adj, L0_gnn_w_self, L0_gnn_w_neigh, L1_gnn_W_self, L1_gnn_b_self, L1_gnn_W_nb, L1_gnn_b_nb, L1_gnn_W_comb, L1_gnn_b_comb):
    import jax
    import jax.numpy as jnp

    def _L0_gnn_ref(node_feats, adj_matrix, w_self, w_neigh):
        import jax, jax.numpy as jnp
        import numpy as np
        N = 4096
        D_IN = 256
        D_OUT = 256
        adj_f = adj_matrix.astype(node_feats.dtype)
        s = adj_f @ node_feats[:, 0]
        has_neigh = jnp.sum(adj_matrix, axis=1) > 0
        s = jnp.where(has_neigh, s, jnp.zeros_like(s))
        neigh_term = s[:, None] * jnp.sum(w_neigh, axis=1)[None, :]
        return jax.nn.relu(node_feats @ w_self.T + neigh_term)

    def _L1_gnn_ref(x, adj, W_self, b_self, W_nb, b_nb, W_comb, b_comb):
        import jax, jax.numpy as jnp
        import numpy as np
        N, D_IN, D_OUT = (4096, 256, 256)
        mask = (adj > 0).astype(x.dtype)
        deg = jnp.sum(mask, axis=1, keepdims=True)
        agg = mask @ x / jnp.maximum(deg, 1.0)
        self_f = x @ W_self + b_self
        nb_f = agg @ W_nb + b_nb
        combined = jnp.concatenate([self_f, nb_f], axis=-1)
        out = combined @ W_comb + b_comb
        return jax.nn.relu(out)
    x = _layernorm(x + _L0_gnn_ref(x, adj, L0_gnn_w_self, L0_gnn_w_neigh), axis=-1)
    x = _layernorm(x + _L1_gnn_ref(x, adj, L1_gnn_W_self, L1_gnn_b_self, L1_gnn_W_nb, L1_gnn_b_nb, L1_gnn_W_comb, L1_gnn_b_comb), axis=-1)
    return x

_drawn_inputs = setup_inputs


def setup_inputs(seed=0):
    import zlib

    import numpy as np

    out = dict(_drawn_inputs(seed))
    spreads = {}
    factors = {'L1_gnn_b_self': 6.279, 'L1_gnn_b_nb': 5.302, 'L1_gnn_b_comb': 3.203}
    for name, (base, spread) in spreads.items():
        noise = np.random.default_rng([zlib.crc32(name.encode()), seed]).standard_normal(out[name].shape)
        drawn = base * np.exp(spread * noise) if base else spread * noise
        out[name] = jnp.asarray(drawn.astype(out[name].dtype))
    for name, factor in factors.items():
        out[name] = (out[name] * factor).astype(out[name].dtype)
    return out
```

```python
from contextlib import ExitStack

import concourse.bass as bass
from concourse import mybir
from concourse.alu_op_type import AluOpType as ALU

ACT = mybir.ActivationFunctionType
F32 = mybir.dt.float32
F16 = mybir.dt.float16
BF16 = mybir.dt.bfloat16
FP8 = mybir.dt.float8e4
I32 = mybir.dt.int32
U8 = mybir.dt.uint8

P = 128
N = 4096
D = 256
DH = D // P
IW = 512
GROUPS = N // IW
TPG = IW // P
JT = N // P
CT = 2
CHUNKS = JT // CT
SLOTS = 4
SCALE = 2.0 ** 11
EPS = 1e-5
ONE_FP8 = 56.0
SREP = 32
BN = 6


def build(nc, adjT, xtile, xT, xcol, w0T, wnT, wsT, wbT, wc, bcol, bcomb, ident_d, comb_d, sel_d, out):
    with ExitStack() as ctx:
        def sb(name, shape, dt):
            return ctx.enter_context(nc.sbuf_tensor(name, shape, dt))

        def sem(name):
            return ctx.enter_context(nc.semaphore(name))

        mask = sb("mask", [P, GROUPS * JT * IW], U8)
        mask8 = mask[:, :].bitcast(FP8)
        part32 = mask[:, :].bitcast(F32)
        ROW32 = JT * IW // 4
        x1hl = sb("x1hl", [P, JT * 2 * D], F16)
        ARENA = 8192
        arena = sb("arena", [P, ARENA], F32)
        SLOTW = CT * IW
        stage = [arena[:, k * SLOTW:(k + 1) * SLOTW].bitcast(I32) for k in range(SLOTS)]
        GD = TPG * D
        x0 = arena[:, SLOTS * SLOTW:SLOTS * SLOTW + GD]
        x0T = arena[:, SLOTS * SLOTW + GD:SLOTS * SLOTW + 2 * GD]
        x1s = arena[:, SLOTS * SLOTW + 2 * GD:SLOTS * SLOTW + 3 * GD]
        aggT = [arena[:, k * DH * IW:(k + 1) * DH * IW] for k in range(2)]
        x1f = [arena[:, 2 * GD + k * GD:3 * GD + k * GD] for k in range(2)]
        z = [arena[:, 4 * GD + k * GD:5 * GD + k * GD] for k in range(2)]
        x1T = arena[:, 6 * GD:7 * GD]
        selfb = [arena[:, 7 * GD + k * D:7 * GD + (k + 1) * D] for k in range(2)]
        w0 = sb("w0", [P, DH * D], F32)
        wself = sb("wself", [P, DH * D], F32)
        wnb = sb("wnb", [P, DH * D], F32)
        wnsum = sb("wnsum", [P, D], F32)
        bias3 = sb("bias3", [3, D], BF16)
        ones3 = sb("ones3", [3, P], BF16)
        ident = sb("ident", [P, P], F32)
        comb = sb("comb", [P, 2], F32)
        xs = sb("xs", [P, JT * SREP], BF16)
        xc = sb("xc", [P, JT], F32)
        srow = sb("srow", [P, IW], F32)
        sdeg = sb("sdeg", [P, 2 * TPG], F32)
        scol = sb("scol", [P, TPG], F32)
        dmax = sb("dmax", [P, TPG], F32)
        rdeg = sb("rdeg", [P, JT], F32)
        stats = sb("stats", [P, TPG * BN], F32)
        mv = sb("mv", [P, TPG * 2], F32)
        ve = sb("ve", [P, TPG], F32)
        sd = sb("sd", [P, TPG], F32)
        r0 = sb("r0", [P, TPG], F32)
        rt = sb("rt", [P, TPG], F32)
        rstd = sb("rstd", [P, TPG], F32)
        raw = x1hl[:, 12 * 2 * D:].bitcast(F32)
        wn_r = raw[:, 0:DH * D]
        ws_r = raw[:, DH * D:2 * DH * D]
        wb_r = raw[:, 2 * DH * D:3 * DH * D]
        wc_r = raw[:, 3 * DH * D:5 * DH * D]
        bc_r = raw[:, 5 * DH * D:5 * DH * D + 12]
        ones_r = raw[:, 5 * DH * D + 12:5 * DH * D + 12 + P]
        bcomb_r = raw[0:3, 6 * DH * D:6 * DH * D + D]
        bsum = raw[0:3, 6 * DH * D + D:6 * DH * D + 2 * D]
        brem = raw[0:3, 7 * DH * D:7 * DH * D + D]
        bacc = raw[0:3, 7 * DH * D + D:7 * DH * D + 2 * D]
        sel = raw[0:3, 8 * DH * D:8 * DH * D + 3]
        bpart = x1hl[0:3, 10 * 2 * D:10 * 2 * D + D].bitcast(BF16)
        xrem = raw[:, 9 * DH * D:9 * DH * D + JT]

        def ps(name, banks):
            return ctx.enter_context(nc.psum_tensor(name, [P, banks * 512], F32))
        acc0 = ps("acc0", 2)
        work = ps("work", 2)
        fin = ps("fin", 2)
        psS = ps("psS", 1)
        psX = ps("psX", 1)

        names = """const_in b_in raw_in adj0 adj1 adj2 adj3 x0_in x0T_in ones_set xs_ready
            wprod_ready wprod_taken bias_ready mask_ready l0_ready s_ready srow_ready comb_ready
            comb_taken scol_ready guard_in rdeg_ready pre_ready u_ready st_ready mv_ready ve_ready sd_ready
            r_steps rstd_ready x1s_ready hi_ready lo_ready sum_ready part_ready acc0_ready
            x1f_ready xt_ready x1T_ready agg_ready sum2_ready fin_ready selfb_ready v_ready z_ready st2_ready
            mv2_ready ve2_ready sd2_ready r2_steps rstd2_ready out_ready out_done0 out_done1 prep dmax_ready""".split()
        S = {n: sem(n) for n in names}
        adj_in = [S["adj%d" % k] for k in range(SLOTS)]
        out_done = [S["out_done%d" % k] for k in range(2)]

        block = ctx.enter_context(nc.Block())

        @block.sync
        def _(sp):
            def load(chunk, slot):
                sp.dma_start(stage[slot], adjT[bass.ds(chunk, 1), :, :].rearrange("c p n -> p (c n)")
                             ).then_inc(adj_in[slot], 16)

            for s in range(SLOTS):
                load(s, s)
            with sp.Fori(1, GROUPS * CHUNKS // SLOTS) as m:
                for s in range(SLOTS):
                    sp.wait_ge(S["mask_ready"], m * SLOTS + (s + 1 - SLOTS))
                    load(m * SLOTS + s, s)
            for n, g in enumerate(FINAL_ORDER):
                sp.wait_ge(S["out_ready"], TPG * (n + 1))
                sp.dma_start(out[g], z[n % 2]).then_inc(out_done[n % 2], 16)
            for b in range(2):
                sp.wait_ge(out_done[b], 16 * (GROUPS // 2))

        @block.gpsimd
        def _(pool):
            for n, g in enumerate(FINAL_ORDER):
                if n == 0:
                    pool.wait_ge(S["lo_ready"], JT)
                if n >= 2:
                    pool.wait_ge(S["z_ready"], TPG * (n - 1))
                    pool.wait_ge(S["xt_ready"], 2 * (n - 1))
                for k in range(TPG):
                    o = (g * TPG + k) * 2 * D
                    nc.gpsimd.tensor_tensor(x1f[n % 2][:, k * D:(k + 1) * D], x1hl[:, o:o + D],
                                            x1hl[:, o + D:o + 2 * D], ALU.add).then_inc(S["x1f_ready"], 1)

        @block.scalar
        def _(act):
            act.dma_start(x0T, xT[0]).then_inc(S["x0T_in"], 16)
            act.dma_start(x0, xtile[0]).then_inc(S["x0_in"], 16)
            act.dma_start(xc[:, :], xcol).then_inc(S["const_in"], 16)
            act.dma_start(w0[:, :], w0T).then_inc(S["const_in"], 16)
            act.dma_start(ident[:, :], ident_d).then_inc(S["const_in"], 16)
            act.dma_start(comb[:, :], comb_d).then_inc(S["const_in"], 16)
            act.dma_start(wn_r, wnT).then_inc(S["raw_in"], 16)
            act.dma_start(ws_r, wsT).then_inc(S["raw_in"], 16)
            act.dma_start(wb_r, wbT).then_inc(S["raw_in"], 16)
            act.dma_start(wc_r, wc).then_inc(S["raw_in"], 16)
            act.dma_start(bc_r, bcol).then_inc(S["raw_in"], 16)
            act.dma_start(bcomb_r, bcomb).then_inc(S["b_in"], 16)
            act.dma_start(sel, sel_d).then_inc(S["b_in"], 16)

            act.wait_ge(S["wprod_ready"], 1)
            nc.scalar.copy(wnsum[:, :], acc0[:, 0:D]).then_inc(S["wprod_taken"], 1)
            act.wait_ge(S["wprod_ready"], 2)
            nc.scalar.copy(wself[:, :], work[:, 0:DH * D]).then_inc(S["wprod_taken"], 1)
            act.wait_ge(S["wprod_ready"], 3)
            nc.scalar.copy(wnb[:, :], work[:, 512:512 + DH * D]).then_inc(S["wprod_taken"], 1)

            def partial(g):
                act.wait_ge(S["sum_ready"], g)
                nc.scalar.copy(part32[:, bass.ds(g * ROW32, DH * IW)], work[:, :]).then_inc(S["part_ready"], 1)

            def layer0(g):
                act.wait_ge(S["s_ready"], g + 1)
                nc.scalar.copy(srow[:, :], psS[:, :]).then_inc(S["srow_ready"], 1)
                act.wait_ge(S["ve_ready"], g + 1)
                nc.scalar.activation(sd[:, :], ve[:, :], ACT.Sqrt).then_inc(S["sd_ready"], 1)
                for k in range(TPG):
                    act.wait_ge(S["x1s_ready"], g * TPG + k + 1)
                    nc.scalar.copy(x1hl[:, bass.ds((g * TPG + k) * 2 * D, D)],
                                   x1s[:, k * D:(k + 1) * D]).then_inc(S["hi_ready"], 1)

            def next_x(g):
                act.wait_ge(S["l0_ready"], g + 1)
                act.dma_start(x0T, xT[bass.ds(g + 1, 1)].rearrange("c p n -> p (c n)")
                              ).then_inc(S["x0T_in"], 16)
                act.wait_ge(S["x1s_ready"], TPG * g + TPG)
                act.dma_start(x0, xtile[bass.ds(g + 1, 1)].rearrange("c p n -> p (c n)")
                              ).then_inc(S["x0_in"], 16)

            layer0(0)
            next_x(0)
            layer0(1)
            next_x(1)
            with act.Fori(2, GROUPS - 1) as g:
                partial(g - 1)
                layer0(g)
                next_x(g)
            partial(GROUPS - 2)
            layer0(GROUPS - 1)

            def transposed(n):
                for h in range(2):
                    act.wait_ge(S["xt_ready"], 2 * n + h + 1)
                    if n >= 1 and h == 0:
                        act.wait_ge(S["fin_ready"], TPG * n)
                    if n == 0 and h == 0:
                        act.wait_ge(S["lo_ready"], JT)
                    bank = psS if h == 0 else psX
                    nc.scalar.copy(x1T[:, h * 512:(h + 1) * 512], bank[:, :]).then_inc(S["x1T_ready"], 1)

            def self_parts(n):
                for k in range(TPG):
                    t = n * TPG + k
                    act.wait_ge(S["fin_ready"], t + 1)
                    if t >= 2:
                        act.wait_ge(S["v_ready"], t - 1)
                    nc.scalar.copy(selfb[t % 2], fin[:, (t % 2) * 512 + D:(t % 2) * 512 + 2 * D]
                                   ).then_inc(S["selfb_ready"], 1)
                act.wait_ge(S["ve2_ready"], n + 1)
                nc.scalar.activation(sd[:, :], ve[:, :], ACT.Sqrt).then_inc(S["sd2_ready"], 1)

            for n in range(GROUPS):
                transposed(n)
                self_parts(n)

        @block.vector
        def _(dve):
            nc.vector.memset(xs[:, :], 0.0).then_inc(S["prep"], 1)
            nc.vector.memset(ones3[:, :], 1.0).then_inc(S["ones_set"], 1)
            nc.vector.memset(ones_r, 1.0).then_inc(S["ones_set"], 1)
            xsv = xs[:, :].rearrange("p (j c) -> p c j", c=SREP)
            dve.wait_ge(S["const_in"], 64)
            dve.wait_ge(S["prep"], 1)
            nc.vector.tensor_copy(xsv[:, 0, :], xc[:, :]).then_inc(S["prep"], 1)
            dve.wait_ge(S["prep"], 2)
            nc.vector.tensor_tensor(xc[:, :], xc[:, :], xsv[:, 0, :], ALU.subtract).then_inc(S["prep"], 1)
            dve.wait_ge(S["prep"], 3)
            nc.vector.tensor_copy(xsv[:, 1, :], xc[:, :]).then_inc(S["prep"], 1)
            dve.wait_ge(S["prep"], 4)
            nc.vector.tensor_tensor(xc[:, :], xc[:, :], xsv[:, 1, :], ALU.subtract).then_inc(S["prep"], 1)
            dve.wait_ge(S["prep"], 5)
            nc.vector.tensor_copy(xsv[:, 2, :], xc[:, :]).then_inc(S["xs_ready"], 1)
            nc.vector.memset(xsv[:, 3, :], 1.0).then_inc(S["xs_ready"], 1)

            dve.wait_ge(S["b_in"], 32)
            dve.wait_ge(S["wprod_ready"], 4)
            nc.vector.tensor_tensor(bsum, psX[0:3, 0:D], bcomb_r, ALU.add).then_inc(S["prep"], 1)
            dve.wait_ge(S["prep"], 6)
            nc.vector.tensor_scalar(brem, bsum, SCALE, None, ALU.mult).then_inc(S["prep"], 1)
            dve.wait_ge(S["prep"], 7)
            nc.vector.tensor_copy(bpart, brem).then_inc(S["prep"], 1)
            dve.wait_ge(S["prep"], 8)
            nc.vector.tensor_scalar(bacc, bpart, sel[:, 0:1], None, ALU.mult).then_inc(S["prep"], 1)
            for m in range(1, 3):
                dve.wait_ge(S["prep"], 4 * m + 5)
                nc.vector.tensor_tensor(brem, brem, bpart, ALU.subtract).then_inc(S["prep"], 1)
                dve.wait_ge(S["prep"], 4 * m + 6)
                nc.vector.tensor_copy(bpart, brem).then_inc(S["prep"], 1)
                dve.wait_ge(S["prep"], 4 * m + 7)
                nc.vector.scalar_tensor_tensor(out=bacc, in0=bpart, scalar=sel[:, m:m + 1], in1=bacc,
                                               op0=ALU.mult, op1=ALU.add).then_inc(S["prep"], 1)
                dve.wait_ge(S["prep"], 4 * m + 8)
                nc.vector.tensor_copy(bias3[:, :], bacc).then_inc(S["prep"], 1)
            dve.wait_ge(S["prep"], 17)

            def to_mask(g, c):
                slot = c % SLOTS
                dve.wait_ge(adj_in[slot], g * (16 * CHUNKS // SLOTS) + 16 * (c // SLOTS + 1))
                nc.vector.tensor_scalar(mask[:, bass.ds(g * (JT * IW) + c * CT * IW, CT * IW)], stage[slot],
                                        0.0, ONE_FP8, ALU.is_gt, ALU.mult).then_inc(S["mask_ready"], 1)

            def degrees(g):
                dve.wait_ge(S["comb_ready"], g + 1)
                nc.vector.tensor_copy(sdeg[:, :], psX[:, 0:2 * TPG]).then_inc(S["comb_taken"], 1)
                dve.wait_ge(S["comb_taken"], g + 1)
                sv = sdeg[:, :].rearrange("p (k c) -> p c k", c=2)
                nc.vector.scalar_tensor_tensor(out=scol[:, :], in0=sv[:, 1, :], scalar=0.0, in1=sv[:, 0, :],
                                               op0=ALU.is_gt, op1=ALU.mult).then_inc(S["scol_ready"], 1)
                nc.vector.tensor_scalar(dmax[:, :], sv[:, 1, :], 1.0, None, ALU.max).then_inc(S["dmax_ready"], 1)

            def pre_act(g, k):
                if k == 0:
                    dve.wait_ge(S["l0_ready"], g + 1)
                    dve.wait_ge(S["scol_ready"], g + 1)
                nc.vector.scalar_tensor_tensor(out=x1s[:, k * D:(k + 1) * D], in0=wnsum[:, :],
                                               scalar=scol[:, k:k + 1], in1=fin[:, k * D:(k + 1) * D],
                                               op0=ALU.mult, op1=ALU.add).then_inc(S["pre_ready"], 1)

            def residual(g, k):
                if k == 0:
                    dve.wait_ge(S["x0_in"], g * 16 + 16)
                dve.wait_ge(S["pre_ready"], g * TPG + k + 1)
                nc.vector.scalar_tensor_tensor(out=x0[:, k * D:(k + 1) * D], in0=x1s[:, k * D:(k + 1) * D],
                                               scalar=0.0, in1=x0[:, k * D:(k + 1) * D],
                                               op0=ALU.max, op1=ALU.add).then_inc(S["u_ready"], 1)

            def halves(src, k, value, count, done):
                dve.wait_ge(value, count)
                nc.vector.bn_stats(stats[:, k * BN:(k + 1) * BN], src).then_inc(done, 1)

            def moments(last):
                for k in range(TPG):
                    nc.vector.bn_aggr(mv[:, 2 * k:2 * k + 2], stats[:, k * BN:(k + 1) * BN]).then_inc(last, 1)

            var = mv[:, :].rearrange("p (k c) -> p c k", c=2)[:, 1, :]

            def inv_std(g, gain, eps, mv_s, ve_s, sd_s, steps, done):
                dve.wait_ge(mv_s, g * TPG + TPG)
                nc.vector.tensor_scalar(ve[:, :], var, eps, None, ALU.add).then_inc(ve_s, 1)
                dve.wait_ge(sd_s, g + 1)
                nc.vector.reciprocal(r0[:, :], sd[:, :]).then_inc(steps, 1)
                dve.wait_ge(steps, g * 4 + 1)
                nc.vector.tensor_tensor(rt[:, :], r0[:, :], r0[:, :], ALU.mult).then_inc(steps, 1)
                dve.wait_ge(steps, g * 4 + 2)
                nc.vector.tensor_tensor(rt[:, :], rt[:, :], ve[:, :], ALU.mult).then_inc(steps, 1)
                dve.wait_ge(steps, g * 4 + 3)
                nc.vector.tensor_scalar(rt[:, :], rt[:, :], -0.5, 1.5, ALU.mult, ALU.add).then_inc(steps, 1)
                dve.wait_ge(steps, g * 4 + 4)
                nc.vector.scalar_tensor_tensor(out=rstd[:, :], in0=r0[:, :], scalar=gain, in1=rt[:, :],
                                               op0=ALU.mult, op1=ALU.mult).then_inc(done, 1)

            def layer0_norm(g):
                inv_std(g, SCALE, EPS, S["mv_ready"], S["ve_ready"], S["sd_ready"], S["r_steps"],
                        S["rstd_ready"])
                dve.wait_ge(S["rstd_ready"], g + 1)
                for k in range(TPG):
                    nc.vector.tensor_scalar(x1s[:, k * D:(k + 1) * D], x0[:, k * D:(k + 1) * D],
                                            mv[:, 2 * k:2 * k + 1], rstd[:, k:k + 1], ALU.subtract, ALU.mult
                                            ).then_inc(S["x1s_ready"], 1)
                for k in range(TPG):
                    dve.wait_ge(S["hi_ready"], g * TPG + k + 1)
                    o = (g * TPG + k) * 2 * D
                    nc.vector.tensor_tensor(x1hl[:, bass.ds(o + D, D)], x1s[:, k * D:(k + 1) * D],
                                            x1hl[:, bass.ds(o, D)], ALU.subtract).then_inc(S["lo_ready"], 1)

            dve.wait_ge(S["wprod_taken"], 1)
            with dve.Fori(0, GROUPS) as g:
                for c in range(CHUNKS):
                    to_mask(g, c)
                degrees(g)
                for k in range(TPG):
                    pre_act(g, k)
                for k in range(TPG):
                    residual(g, k)
                for k in range(TPG):
                    halves(x0[:, k * D:(k + 1) * D], k, S["u_ready"], g * TPG + k + 1, S["st_ready"])
                dve.wait_ge(S["dmax_ready"], g + 1)
                dve.wait_ge(S["st_ready"], g * TPG + TPG)
                nc.vector.reciprocal(rdeg[:, bass.ds(g * TPG, TPG)], dmax[:, :]).then_inc(S["rdeg_ready"], 1)
                moments(S["mv_ready"])
                layer0_norm(g)

            def gather(n, g):
                if n >= 2:
                    dve.wait_ge(S["fin_ready"], TPG * (n - 1))
                if g == GROUPS - 1:
                    dve.wait_ge(S["sum_ready"], g)
                    dve.wait_ge(S["lo_ready"], JT)
                    nc.vector.tensor_copy(aggT[n % 2], work[:, :]).then_inc(S["agg_ready"], 1)
                elif g == 0:
                    dve.wait_ge(S["acc0_ready"], 1)
                    nc.vector.tensor_copy(aggT[n % 2], acc0[:, :]).then_inc(S["agg_ready"], 1)
                else:
                    dve.wait_ge(S["sum2_ready"], g)
                    dve.wait_ge(S["part_ready"], g)
                    bank = work if g % 2 else acc0
                    nc.vector.tensor_tensor(aggT[n % 2], bank[:, :], part32[:, g * ROW32:g * ROW32 + DH * IW],
                                            ALU.add).then_inc(S["agg_ready"], 1)

            def layer1(n, g):
                zn = z[n % 2]
                if n >= 2:
                    dve.wait_ge(out_done[n % 2], 16 * (n // 2))
                for k in range(TPG):
                    t = n * TPG + k
                    dve.wait_ge(S["selfb_ready"], t + 1)
                    if t == 0:
                        dve.wait_ge(S["rdeg_ready"], GROUPS)
                    nc.vector.scalar_tensor_tensor(
                        out=zn[:, k * D:(k + 1) * D], in0=fin[:, (t % 2) * 512:(t % 2) * 512 + D],
                        scalar=rdeg[:, g * TPG + k:g * TPG + k + 1], in1=selfb[t % 2],
                        op0=ALU.mult, op1=ALU.add).then_inc(S["v_ready"], 1)
                    dve.wait_ge(S["v_ready"], t + 1)
                    dve.wait_ge(S["x1f_ready"], t + 1)
                    nc.vector.scalar_tensor_tensor(
                        out=zn[:, k * D:(k + 1) * D], in0=zn[:, k * D:(k + 1) * D], scalar=0.0,
                        in1=x1f[n % 2][:, k * D:(k + 1) * D], op0=ALU.max, op1=ALU.add
                    ).then_inc(S["z_ready"], 1)
                for k in range(TPG):
                    halves(zn[:, k * D:(k + 1) * D], k, S["z_ready"], n * TPG + k + 1, S["st2_ready"])
                dve.wait_ge(S["st2_ready"], n * TPG + TPG)
                moments(S["mv2_ready"])

            def layer1_norm(n):
                zn = z[n % 2]
                inv_std(n, 1.0, EPS * SCALE * SCALE, S["mv2_ready"], S["ve2_ready"], S["sd2_ready"],
                        S["r2_steps"], S["rstd2_ready"])
                dve.wait_ge(S["rstd2_ready"], n + 1)
                for k in range(TPG):
                    nc.vector.tensor_scalar(zn[:, k * D:(k + 1) * D], zn[:, k * D:(k + 1) * D],
                                            mv[:, 2 * k:2 * k + 1], rstd[:, k:k + 1], ALU.subtract, ALU.mult
                                            ).then_inc(S["out_ready"], 1)

            gather(0, FINAL_ORDER[0])
            gather(1, FINAL_ORDER[1])
            for n, g in enumerate(FINAL_ORDER):
                layer1(n, g)
                layer1_norm(n)
                if n + 2 < GROUPS:
                    gather(n + 2, FINAL_ORDER[n + 2])

        @block.tensor
        def _(pe):
            mm = nc.tensor.matmul

            def fold(dst, lhs, rhs0):
                for h in range(DH):
                    for m in range(DH):
                        last = mm(dst[:, h * D:(h + 1) * D], lhs[:, m * D + h * P:m * D + (h + 1) * P],
                                  wc_r[:, (rhs0 + m) * D:(rhs0 + m + 1) * D], start=(m == 0), stop=(m == DH - 1))
                last.then_inc(S["wprod_ready"], 1)

            pe.wait_ge(S["ones_set"], 2)
            pe.wait_ge(S["raw_in"], 80)
            for m in range(DH):
                last = mm(acc0[:, 0:D], ones_r, wn_r[:, m * D:(m + 1) * D], start=(m == 0), stop=(m == DH - 1))
            last.then_inc(S["wprod_ready"], 1)
            fold(work[:, 0:512], ws_r, 0)
            fold(work[:, 512:1024], wb_r, DH)
            for m in range(2 * DH):
                last = mm(psX[0:3, 0:D], bc_r[:, 3 * m:3 * m + 3], wc_r[:, m * D:(m + 1) * D],
                          start=(m == 0), stop=(m == 2 * DH - 1))
            last.then_inc(S["wprod_ready"], 1)

            def layer0_products(g):
                pe.wait_ge(S["x0T_in"], 16 * (g + 1))
                if g == 0:
                    pe.wait_ge(S["const_in"], 64)
                else:
                    pe.wait_ge(S["pre_ready"], TPG * g)
                for k in range(TPG):
                    for h in range(DH):
                        last = mm(fin[:, k * D:(k + 1) * D], x0T[:, h * IW + k * P:h * IW + (k + 1) * P],
                                  w0[:, h * D:(h + 1) * D], start=(h == 0), stop=(h == DH - 1))
                last.then_inc(S["l0_ready"], 1)

            def neighbour_sums(g):
                if g == 0:
                    pe.wait_ge(S["xs_ready"], 2)
                else:
                    pe.wait_ge(S["srow_ready"], g)
                for j in range(JT):
                    if j % CT == 0:
                        pe.wait_ge(S["mask_ready"], g * CHUNKS + j // CT + 1)
                    q = j % 4 * SREP
                    last = mm(psS[q:q + SREP, :], xs[:, j * SREP:(j + 1) * SREP],
                              mask8[:, (g * JT + j) * IW:(g * JT + j + 1) * IW],
                              start=(j < 4), stop=(j >= JT - 4), tile_position=(0, q))
                last.then_inc(S["s_ready"], 1)

            def columns(g):
                pe.wait_ge(S["srow_ready"], g + 1)
                if g == 0:
                    pe.wait_ge(S["prep"], 6)
                else:
                    pe.wait_ge(S["comb_taken"], g)
                for k in range(TPG):
                    last = mm(psX[:, 2 * k:2 * k + 2], srow[:, k * P:(k + 1) * P], comb[:, :],
                              start=True, stop=True)
                last.then_inc(S["comb_ready"], 1)

            def aggregate(dst, g, j, start, stop):
                for part in range(2):
                    for h in range(DH):
                        o = (j * 2 + part) * D + h * P
                        last = mm(dst[:, h * IW:(h + 1) * IW], x1hl[:, o:o + P],
                                  mask8[:, (g * JT + j) * IW:(g * JT + j + 1) * IW],
                                  start=(start and part == 0), stop=(stop and part == 1))
                return last

            for g in range(GROUPS):
                layer0_products(g)
                neighbour_sums(g)
                if g == 0:
                    columns(0)
                    pe.wait_ge(S["wprod_taken"], 3)
                else:
                    if g >= 2:
                        pe.wait_ge(S["part_ready"], g - 1)
                    for j in range(TPG * g):
                        if j == TPG // 2:
                            columns(g)
                        aggregate(work, g, j, j == 0, False)
                    for k in range(TPG):
                        pe.wait_ge(S["lo_ready"], TPG * g + k + 1)
                        last = aggregate(work, g, TPG * g + k, False, k == TPG - 1)
                    last.then_inc(S["sum_ready"], 1)
                for k in range(TPG):
                    pe.wait_ge(S["lo_ready"], TPG * g + k + 1)
                    j = TPG * g + k
                    last = aggregate(acc0, 0, j, j == 0, j == JT - 1)
            last.then_inc(S["acc0_ready"], 1)

            def turn_x1(n):
                for h in range(2):
                    bank = psS if h == 0 else psX
                    if n >= 1:
                        pe.wait_ge(S["x1T_ready"], 2 * (n - 1) + h + 1)
                    elif h == 1:
                        pe.wait_ge(S["comb_taken"], GROUPS)
                    pe.wait_ge(S["x1f_ready"], TPG * n + 2 * h + 2)
                    for q in range(4):
                        k, f = 2 * h + q // 2, q % 2
                        last = nc.tensor.transpose(bank[:, q * P:(q + 1) * P],
                                                   x1f[n % 2][:, k * D + f * P:k * D + (f + 1) * P], ident[:, :])
                    last.then_inc(S["xt_ready"], 1)

            def layer1_products(n):
                pe.wait_ge(S["agg_ready"], n + 1)
                if n == 0:
                    pe.wait_ge(S["prep"], 17)
                    pe.wait_ge(S["ones_set"], 2)
                for k in range(TPG):
                    t = n * TPG + k
                    b = (t % 2) * 512
                    if t >= 2:
                        pe.wait_ge(S["v_ready"], t - 1)
                    else:
                        pe.wait_ge(S["pre_ready"], TPG * GROUPS)
                    for h in range(DH):
                        mm(fin[:, b:b + D], aggT[n % 2][:, h * IW + k * P:h * IW + (k + 1) * P],
                           wnb[:, h * D:(h + 1) * D], start=(h == 0), stop=(h == DH - 1))
                    mm(fin[:, b + D:b + 2 * D], ones3[:, :], bias3[:, :], start=True, stop=False)
                    if k % 2 == 0:
                        pe.wait_ge(S["x1T_ready"], 2 * n + k // 2 + 1)
                    for h in range(DH):
                        last = mm(fin[:, b + D:b + 2 * D], x1T[:, (2 * k + h) * P:(2 * k + h + 1) * P],
                                  wself[:, h * D:(h + 1) * D], start=False, stop=(h == DH - 1))
                    last.then_inc(S["fin_ready"], 1)

            turn_x1(0)
            layer1_products(0)
            for g in range(1, GROUPS - 1):
                turn_x1(g)
                pe.wait_ge(S["agg_ready"], g)
                for j in range(TPG * (g + 1), JT):
                    last = aggregate(work if g % 2 else acc0, g, j, j == TPG * (g + 1), j == JT - 1)
                last.then_inc(S["sum2_ready"], 1)
                layer1_products(g)
            turn_x1(GROUPS - 1)
            layer1_products(GROUPS - 1)


FINAL_ORDER = [GROUPS - 1] + list(range(GROUPS - 1))


def kernel(**inputs):
    import numpy as _np
    import concourse.bacc as _bacc
    from concourse import mybir as _mybir
    from concourse.bass_utils import run_bass_kernel_spmd as _run

    a = {k: _np.asarray(v) for k, v in inputs.items()}
    x = a["x"]
    rows = lambda w, t: w.reshape(t, P, -1).transpose(1, 0, 2).reshape(P, -1)
    bias = _np.concatenate([a["L1_gnn_b_self"], a["L1_gnn_b_nb"]]).reshape(2 * DH, P)
    comb = _np.zeros((P, 2), _np.float32)
    for q in range(4):
        comb[q * SREP:q * SREP + 3, 0] = 1.0
        comb[q * SREP + 3, 1] = 1.0
    arrays = {
        "adjT": a["adj"].reshape(GROUPS, IW, CHUNKS, CT, P).transpose(0, 2, 4, 3, 1)
                        .reshape(GROUPS * CHUNKS, P, CT * IW),
        "xtile": x.reshape(GROUPS, TPG, P, D).transpose(0, 2, 1, 3).reshape(GROUPS, P, TPG * D),
        "xT": x.T.reshape(DH, P, GROUPS, IW).transpose(2, 1, 0, 3).reshape(GROUPS, P, DH * IW),
        "xcol": x[:, 0].reshape(JT, P).T,
        "w0T": rows(a["L0_gnn_w_self"].T, DH),
        "wnT": rows(a["L0_gnn_w_neigh"].T, DH),
        "wsT": rows(a["L1_gnn_W_self"].T, DH),
        "wbT": rows(a["L1_gnn_W_nb"].T, DH),
        "wc": rows(a["L1_gnn_W_comb"], 2 * DH),
        "bcol": _np.repeat(bias.T, 3, axis=1),
        "bcomb": _np.broadcast_to(a["L1_gnn_b_comb"], (3, D)),
        "ident": _np.eye(P, dtype=_np.float32),
        "comb": comb,
        "sel": _np.eye(3, dtype=_np.float32),
    }
    arrays = {k + "_dram": _np.ascontiguousarray(v) for k, v in arrays.items()}
    nc = _bacc.Bacc("TRN2", target_bir_lowering=False, num_devices=1)
    args = [nc.dram_tensor(k, v.shape, _mybir.dt.from_np(v.dtype), kind="ExternalInput").ap()
            for k, v in arrays.items()]
    out = nc.dram_tensor("out_dram", (GROUPS, P, TPG * D), F32, kind="ExternalOutput").ap()
    build(nc, *args, out)
    r = _run(nc, [arrays], core_ids=[0]).results[0]["out_dram"]
    return r.reshape(GROUPS, P, TPG, D).transpose(0, 2, 1, 3).reshape(N, D)
```

```python
from contextlib import ExitStack

import concourse.bass as bass
from concourse import mybir
from concourse.alu_op_type import AluOpType as ALU

ACT = mybir.ActivationFunctionType
F32 = mybir.dt.float32
F16 = mybir.dt.float16
BF16 = mybir.dt.bfloat16
FP8 = mybir.dt.float8e4
I32 = mybir.dt.int32
U8 = mybir.dt.uint8

P = 128
N = 4096
D = 256
DH = D // P
IW = 512
GROUPS = N // IW
TPG = IW // P
JT = N // P
CT = 2
CHUNKS = JT // CT
SLOTS = 4
AHEAD = 6
RSQRT_SEED = float(0x5F3759DF)
SCALE = 2.0 ** 11
EPS = 1e-5
ONE_FP8 = 56.0
SREP = 32
BN = 6
NEWTON = 3
INV_STEPS = 4 + 3 * NEWTON


def build(nc, adjT, xtile, xT, xcol, w0T, wnT, wsT, wbT, wc, bcol, bcomb, ident_d, comb_d, sel_d, out):
    with ExitStack() as ctx:
        def sb(name, shape, dt):
            return ctx.enter_context(nc.sbuf_tensor(name, shape, dt))

        def sem(name):
            return ctx.enter_context(nc.semaphore(name))

        mask = sb("mask", [P, GROUPS * JT * IW], U8)
        mask8 = mask[:, :].bitcast(FP8)
        part32 = mask[:, :].bitcast(F32)
        ROW32 = JT * IW // 4

        def sums(g):
            return part32[:, bass.ds(g * ROW32, DH * IW)]

        x1hl = sb("x1hl", [P, JT * 2 * D], F16)
        ARENA = 7168
        arena = sb("arena", [P, ARENA], F32)
        SLOTW = CT * IW
        stage = [arena[:, k * SLOTW:(k + 1) * SLOTW].bitcast(I32) for k in range(SLOTS)]
        GD = TPG * D
        x0 = arena[:, SLOTS * SLOTW:SLOTS * SLOTW + GD]
        x0T = arena[:, SLOTS * SLOTW + GD:SLOTS * SLOTW + 2 * GD]
        x1s = arena[:, SLOTS * SLOTW + 2 * GD:SLOTS * SLOTW + 3 * GD]
        x1f = [arena[:, k * GD:(k + 1) * GD] for k in range(2)]
        z = [arena[:, 2 * GD + k * GD:3 * GD + k * GD] for k in range(2)]
        x1T = arena[:, 4 * GD:5 * GD]
        selfb = [arena[:, 5 * GD + k * D:5 * GD + (k + 1) * D] for k in range(2)]
        w0 = sb("w0", [P, DH * D], F32)
        wself = sb("wself", [P, DH * D], F32)
        wnb = sb("wnb", [P, DH * D], F32)
        wnsum = sb("wnsum", [P, D], F32)
        bias3 = sb("bias3", [3, D], BF16)
        ones3 = sb("ones3", [3, P], BF16)
        ident = sb("ident", [P, P], F32)
        comb = sb("comb", [P, 2], F32)
        xs = sb("xs", [P, JT * SREP], BF16)
        xc = sb("xc", [P, JT], F32)
        srow = sb("srow", [P, IW], F32)
        sdeg = sb("sdeg", [P, 2 * TPG], F32)
        scol = sb("scol", [P, TPG], F32)
        dmax = sb("dmax", [P, TPG], F32)
        rdeg = sb("rdeg", [P, JT], F32)
        stats = sb("stats", [P, TPG * BN], F32)
        mv = sb("mv", [P, TPG * 2], F32)
        ve = sb("ve", [P, TPG], F32)
        sd = sb("sd", [P, TPG], F32)
        r0 = sb("r0", [P, TPG], F32)
        rt = sb("rt", [P, TPG], F32)
        rstd = sb("rstd", [P, TPG], F32)
        raw = x1hl[:, 12 * 2 * D:].bitcast(F32)
        wn_r = raw[:, 0:DH * D]
        ws_r = raw[:, DH * D:2 * DH * D]
        wb_r = raw[:, 2 * DH * D:3 * DH * D]
        wc_r = raw[:, 3 * DH * D:5 * DH * D]
        bc_r = raw[:, 5 * DH * D:5 * DH * D + 12]
        ones_r = raw[:, 5 * DH * D + 12:5 * DH * D + 12 + P]
        bcomb_r = raw[0:3, 6 * DH * D:6 * DH * D + D]
        bsum = raw[0:3, 6 * DH * D + D:6 * DH * D + 2 * D]
        brem = raw[0:3, 7 * DH * D:7 * DH * D + D]
        bacc = raw[0:3, 7 * DH * D + D:7 * DH * D + 2 * D]
        sel = raw[0:3, 8 * DH * D:8 * DH * D + 3]
        bpart = x1hl[0:3, 10 * 2 * D:10 * 2 * D + D].bitcast(BF16)
        xrem = raw[:, 9 * DH * D:9 * DH * D + JT]

        def ps(name, banks):
            return ctx.enter_context(nc.psum_tensor(name, [P, banks * 512], F32))
        acc0 = ps("acc0", 2)
        acc1 = ps("acc1", 2)
        work = ps("work", 2)
        psS = ps("psS", 1)
        psX = ps("psX", 1)
        fin = acc1

        names = """w0_in comb_in bias_steps bsum_ready xc_in wn_in ident_in const_in b_in raw_in adj0 adj1 adj2 adj3 x0_in x0T_in ones_set xs_ready
            wprod_ready wprod_taken bias_ready mask_ready l0_ready s_ready srow_ready comb_ready
            comb_taken scol_ready guard_in rdeg_ready pre_ready u_ready st_ready mv_ready ve_ready sd_ready
            r_steps rstd_ready x1s_ready hi_ready lo_ready sum_ready part_ready acc0_ready
            x1f_ready xt_ready x1T_ready agg_ready sum2_ready fin_ready selfb_ready v_ready z_ready st2_ready
            mv2_ready ve2_ready sd2_ready r2_steps rstd2_ready out_ready acc1_ready whole1_ready out_done0 out_done1 prep dmax_ready""".split()
        S = {n: sem(n) for n in names}
        adj_in = [S["adj%d" % k] for k in range(SLOTS)]
        out_done = [S["out_done%d" % k] for k in range(2)]

        block = ctx.enter_context(nc.Block())

        @block.sync
        def _(sp):
            def load(chunk, slot):
                sp.dma_start(stage[slot], adjT[bass.ds(chunk, 1), :, :].rearrange("c p n -> p (c n)")
                             ).then_inc(adj_in[slot], 16)

            for s in range(SLOTS):
                load(s, s)
            with sp.Fori(1, GROUPS * CHUNKS // SLOTS) as m:
                for s in range(SLOTS):
                    sp.wait_ge(S["mask_ready"], m * SLOTS + (s + 1 - SLOTS))
                    load(m * SLOTS + s, s)
            for n, g in enumerate(FINAL_ORDER):
                for h in range(2):
                    sp.wait_ge(S["out_ready"], TPG * n + 2 * h + 2)
                    sp.dma_start(out[g][:, h * 2 * D:(h + 1) * 2 * D], z[n % 2][:, h * 2 * D:(h + 1) * 2 * D]
                                 ).then_inc(out_done[n % 2], 16)
            for b in range(2):
                sp.wait_ge(out_done[b], 32 * (GROUPS // 2))

        @block.gpsimd
        def _(pool):
            pool.dma_start(xc[:, :], xcol).then_inc(S["xc_in"], 16)
            pool.dma_start(w0[:, :], w0T).then_inc(S["w0_in"], 16)
            pool.dma_start(x0T, xT[0]).then_inc(S["x0T_in"], 16)
            pool.dma_start(wn_r, wnT).then_inc(S["wn_in"], 16)
            pool.dma_start(comb[:, :], comb_d).then_inc(S["comb_in"], 16)
            pool.dma_start(x0, xtile[0]).then_inc(S["x0_in"], 16)
            pool.wait_ge(S["mask_ready"], CHUNKS - SLOTS)
            for dst, src in ((ws_r, wsT), (wb_r, wbT), (wc_r, wc), (bc_r, bcol)):
                pool.dma_start(dst, src).then_inc(S["raw_in"], 16)
            pool.dma_start(bcomb_r, bcomb).then_inc(S["b_in"], 16)
            pool.dma_start(sel, sel_d).then_inc(S["b_in"], 16)
            pool.dma_start(ident[:, :], ident_d).then_inc(S["ident_in"], 16)

            def next_x(g):
                pool.wait_ge(S["l0_ready"], 2 * g)
                pool.dma_start(x0T, xT[g]).then_inc(S["x0T_in"], 16)
                pool.wait_ge(S["x1s_ready"], TPG * g)
                pool.dma_start(x0, xtile[g]).then_inc(S["x0_in"], 16)

            next_x(1)

            steps = [0]

            def step(ins):
                steps[0] += 1
                ins.then_inc(S["bias_steps"], 1)
                pool.wait_ge(S["bias_steps"], steps[0])

            pool.wait_ge(S["b_in"], 32)
            pool.wait_ge(S["bsum_ready"], 1)
            step(nc.gpsimd.tensor_tensor(brem, bsum, bcomb_r, ALU.add))
            step(nc.gpsimd.tensor_scalar(brem, brem, SCALE, None, ALU.mult))
            step(nc.gpsimd.tensor_copy(bpart, brem))
            step(nc.gpsimd.tensor_scalar(bacc, bpart, sel[:, 0:1], None, ALU.mult))
            for m in range(1, 3):
                step(nc.gpsimd.tensor_tensor(brem, brem, bpart, ALU.subtract))
                step(nc.gpsimd.tensor_copy(bpart, brem))
                step(nc.gpsimd.tensor_scalar(bsum, bpart, sel[:, m:m + 1], None, ALU.mult))
                step(nc.gpsimd.tensor_tensor(bacc, bacc, bsum, ALU.add))
            nc.gpsimd.tensor_copy(bias3[:, :], bacc).then_inc(S["bias_ready"], 1)

            for g in range(2, GROUPS):
                next_x(g)

            for n, g in enumerate(FINAL_ORDER):
                if n == 0:
                    pool.wait_ge(S["lo_ready"], JT)
                if n >= 2:
                    pool.wait_ge(S["z_ready"], TPG * (n - 1))
                    pool.wait_ge(S["xt_ready"], 2 * (n - 1))
                for k in range(TPG):
                    o = (g * TPG + k) * 2 * D
                    nc.gpsimd.tensor_tensor(x1f[n % 2][:, k * D:(k + 1) * D], x1hl[:, o:o + D],
                                            x1hl[:, o + D:o + 2 * D], ALU.add).then_inc(S["x1f_ready"], 1)

        @block.scalar
        def _(act):
            for g in range(GROUPS):
                for c in range(CHUNKS):
                    act.wait_ge(adj_in[c % SLOTS], 16 * (g * CHUNKS // SLOTS + c // SLOTS + 1))
                    o = (g * JT + c * CT) * IW
                    nc.scalar.activation(mask8[:, o:o + CT * IW], stage[c % SLOTS], ACT.Sign, saturate=False
                                         ).then_inc(S["mask_ready"], 1)
            act.wait_ge(S["acc1_ready"], 1)
            nc.scalar.copy(sums(1), acc1[:, :]).then_inc(S["whole1_ready"], 1)

            def transposed(n):
                for h in range(2):
                    act.wait_ge(S["xt_ready"], 2 * n + h + 1)
                    if n >= 1 and h == 0:
                        act.wait_ge(S["fin_ready"], TPG * n)
                    if n == 0 and h == 0:
                        act.wait_ge(S["lo_ready"], JT)
                    bank = psS if h == 0 else psX
                    nc.scalar.copy(x1T[:, h * 512:(h + 1) * 512], bank[:, :]).then_inc(S["x1T_ready"], 1)

            def self_parts(n):
                for k in range(TPG):
                    t = n * TPG + k
                    act.wait_ge(S["fin_ready"], t + 1)
                    if t >= 2:
                        act.wait_ge(S["v_ready"], t - 1)
                    nc.scalar.copy(selfb[t % 2], fin[:, (t % 2) * 512 + D:(t % 2) * 512 + 2 * D]
                                   ).then_inc(S["selfb_ready"], 1)

            for n in range(GROUPS):
                transposed(n)
                self_parts(n)

        @block.vector
        def _(dve):
            nc.vector.memset(xs[:, :], 0.0).then_inc(S["prep"], 1)
            nc.vector.memset(ones3[:, :], 1.0).then_inc(S["ones_set"], 1)
            nc.vector.memset(ones_r, 1.0).then_inc(S["ones_set"], 1)
            xsv = xs[:, :].rearrange("p (j c) -> p c j", c=SREP)
            dve.wait_ge(S["xc_in"], 16)
            dve.wait_ge(S["prep"], 1)
            nc.vector.tensor_copy(xsv[:, 0, :], xc[:, :]).then_inc(S["prep"], 1)
            dve.wait_ge(S["prep"], 2)
            nc.vector.tensor_tensor(xc[:, :], xc[:, :], xsv[:, 0, :], ALU.subtract).then_inc(S["prep"], 1)
            dve.wait_ge(S["prep"], 3)
            nc.vector.tensor_copy(xsv[:, 1, :], xc[:, :]).then_inc(S["prep"], 1)
            dve.wait_ge(S["prep"], 4)
            nc.vector.tensor_tensor(xc[:, :], xc[:, :], xsv[:, 1, :], ALU.subtract).then_inc(S["prep"], 1)
            dve.wait_ge(S["prep"], 5)
            nc.vector.tensor_copy(xsv[:, 2, :], xc[:, :]).then_inc(S["xs_ready"], 1)
            nc.vector.memset(xsv[:, 3, :], 1.0).then_inc(S["xs_ready"], 1)

            dve.wait_ge(S["wprod_ready"], 1)
            nc.vector.tensor_copy(wnsum[:, :], acc0[:, 0:D]).then_inc(S["wprod_taken"], 1)

            def degrees(g):
                dve.wait_ge(S["s_ready"], g + 1)
                nc.vector.tensor_copy(srow[:, :], psS[:, :]).then_inc(S["srow_ready"], 1)
                dve.wait_ge(S["comb_ready"], g + 1)
                nc.vector.tensor_copy(sdeg[:, :], work[:, 0:2 * TPG]).then_inc(S["comb_taken"], 1)
                dve.wait_ge(S["comb_taken"], g + 1)
                sv = sdeg[:, :].rearrange("p (k c) -> p c k", c=2)
                nc.vector.scalar_tensor_tensor(out=scol[:, :], in0=sv[:, 1, :], scalar=0.0, in1=sv[:, 0, :],
                                               op0=ALU.is_gt, op1=ALU.mult).then_inc(S["scol_ready"], 1)
                nc.vector.tensor_scalar(dmax[:, :], sv[:, 1, :], 1.0, None, ALU.max).then_inc(S["dmax_ready"], 1)

            def pre_act(g, k):
                if k == 2:
                    dve.wait_ge(S["scol_ready"], g + 1)
                if k % 2 == 0:
                    dve.wait_ge(S["l0_ready"], 2 * g + (1 if k == 2 else 2))
                bank = psS if k < 2 else psX
                nc.vector.scalar_tensor_tensor(out=x1s[:, k * D:(k + 1) * D], in0=wnsum[:, :],
                                               scalar=scol[:, k:k + 1],
                                               in1=bank[:, k % 2 * D:(k % 2 + 1) * D],
                                               op0=ALU.mult, op1=ALU.add).then_inc(S["pre_ready"], 1)

            def residual(g, n, k):
                if n == 0:
                    dve.wait_ge(S["x0_in"], g * 16 + 16)
                dve.wait_ge(S["pre_ready"], g * TPG + n + 1)
                nc.vector.scalar_tensor_tensor(out=x0[:, k * D:(k + 1) * D], in0=x1s[:, k * D:(k + 1) * D],
                                               scalar=0.0, in1=x0[:, k * D:(k + 1) * D],
                                               op0=ALU.max, op1=ALU.add).then_inc(S["u_ready"], 1)

            def halves(src, k, value, count, done):
                dve.wait_ge(value, count)
                nc.vector.bn_stats(stats[:, k * BN:(k + 1) * BN], src).then_inc(done, 1)

            def moments(tiles, last):
                for k in tiles:
                    nc.vector.bn_aggr(mv[:, 2 * k:2 * k + 2], stats[:, k * BN:(k + 1) * BN]).then_inc(last, 1)

            var = mv[:, :].rearrange("p (k c) -> p c k", c=2)[:, 1, :]

            def inv_std(call, gain, eps, moments_done, count, steps, done):
                at = call * INV_STEPS
                dve.wait_ge(moments_done, count)
                nc.vector.tensor_scalar(ve[:, :], var, eps, None, ALU.add).then_inc(steps, 1)
                dve.wait_ge(steps, at + 1)
                nc.vector.tensor_scalar(rt[:, :].bitcast(I32), ve[:, :].bitcast(I32), 1, None,
                                        ALU.arith_shift_right).then_inc(steps, 1)
                nc.vector.tensor_scalar(sd[:, :], ve[:, :], -0.5, None, ALU.mult).then_inc(steps, 1)
                dve.wait_ge(steps, at + 3)
                nc.vector.tensor_scalar(r0[:, :].bitcast(I32), rt[:, :].bitcast(I32), -1.0, RSQRT_SEED,
                                        ALU.mult, ALU.add).then_inc(steps, 1)
                for m in range(NEWTON):
                    dve.wait_ge(steps, at + 3 * m + 4)
                    nc.vector.tensor_tensor(rt[:, :], r0[:, :], r0[:, :], ALU.mult).then_inc(steps, 1)
                    dve.wait_ge(steps, at + 3 * m + 5)
                    nc.vector.tensor_tensor(rt[:, :], rt[:, :], sd[:, :], ALU.mult).then_inc(steps, 1)
                    dve.wait_ge(steps, at + 3 * m + 6)
                    nc.vector.scalar_tensor_tensor(out=r0[:, :], in0=rt[:, :], scalar=1.5, in1=r0[:, :],
                                                   op0=ALU.add, op1=ALU.mult).then_inc(steps, 1)
                dve.wait_ge(steps, at + 3 * NEWTON + 4)
                nc.vector.tensor_scalar(rstd[:, :], r0[:, :], gain, None, ALU.mult).then_inc(done, 1)

            def high_low(g, k):
                dve.wait_ge(S["hi_ready"], g * TPG + k + 1)
                o = (g * TPG + k) * 2 * D
                nc.vector.tensor_tensor(x1hl[:, bass.ds(o + D, D)], x1s[:, k * D:(k + 1) * D],
                                        x1hl[:, bass.ds(o, D)], ALU.subtract).then_inc(S["lo_ready"], 1)

            def normalise(k):
                nc.vector.tensor_scalar(x1s[:, k * D:(k + 1) * D], x0[:, k * D:(k + 1) * D],
                                        mv[:, 2 * k:2 * k + 1], rstd[:, k:k + 1], ALU.subtract, ALU.mult
                                        ).then_inc(S["x1s_ready"], 1)

            order = (2, 3, 0, 1)

            def group(g):
                degrees(g)
                for k in order:
                    pre_act(g, k)
                for n, k in enumerate(order):
                    residual(g, n, k)
                for n, k in enumerate(order):
                    halves(x0[:, k * D:(k + 1) * D], k, S["u_ready"], g * TPG + n + 1, S["st_ready"])
                dve.wait_ge(S["dmax_ready"], g + 1)
                dve.wait_ge(S["st_ready"], g * TPG + TPG)
                nc.vector.reciprocal(rdeg[:, bass.ds(g * TPG, TPG)], dmax[:, :]).then_inc(S["rdeg_ready"], 1)
                moments(range(TPG), S["mv_ready"])
                inv_std(g, SCALE, EPS, S["mv_ready"], g * TPG + TPG, S["r_steps"], S["rstd_ready"])
                dve.wait_ge(S["rstd_ready"], g + 1)
                for k in range(TPG):
                    normalise(k)
                for k in range(TPG):
                    dve.wait_ge(S["x1s_ready"], g * TPG + k + 1)
                    nc.vector.tensor_copy(x1hl[:, bass.ds((g * TPG + k) * 2 * D, D)],
                                          x1s[:, k * D:(k + 1) * D]).then_inc(S["hi_ready"], 1)
                for k in range(TPG):
                    high_low(g, k)

            def partial(g):
                dve.wait_ge(S["sum_ready"], g - 1)
                nc.vector.tensor_copy(sums(g), work[:, :]).then_inc(S["part_ready"], 1)

            group(0)
            dve.wait_ge(S["wprod_ready"], 2)
            nc.vector.tensor_copy(wself[:, :], work[:, 0:DH * D]).then_inc(S["wprod_taken"], 1)
            dve.wait_ge(S["wprod_ready"], 3)
            nc.vector.tensor_copy(wnb[:, :], work[:, 512:512 + DH * D]).then_inc(S["wprod_taken"], 1)
            dve.wait_ge(S["wprod_ready"], 4)
            nc.vector.tensor_copy(bsum, acc1[0:3, 0:D]).then_inc(S["bsum_ready"], 1)
            group(1)
            dve.wait_ge(S["bias_ready"], 1)
            with dve.Fori(2, GROUPS - 1) as g:
                group(g)
                partial(g)
            group(GROUPS - 1)

            def gather(n):
                g = FINAL_ORDER[n]
                if n == 0:
                    dve.wait_ge(S["sum_ready"], g - 1)
                    nc.vector.tensor_copy(sums(g), work[:, :]).then_inc(S["agg_ready"], 1)
                elif n == 1:
                    dve.wait_ge(S["acc0_ready"], 1)
                    nc.vector.tensor_copy(sums(g), acc0[:, :]).then_inc(S["agg_ready"], 1)
                else:
                    dve.wait_ge(S["sum2_ready"], n - 2)
                    if n == 3:
                        dve.wait_ge(S["part_ready"], g - 1)
                    nc.vector.tensor_tensor(sums(g), (work if n % 2 else acc0)[:, :], sums(g), ALU.add
                                            ).then_inc(S["agg_ready"], 1)

            def layer1(n, tiles):
                g, zn = FINAL_ORDER[n], z[n % 2]
                for k in tiles:
                    t = n * TPG + k
                    if k == 0 and n >= 2:
                        dve.wait_ge(out_done[n % 2], 32 * (n // 2))
                    if (n, k) == (GROUPS - 2, TPG - 1):
                        gather(n + 1)
                    dve.wait_ge(S["selfb_ready"], t + 1)
                    if t == 0:
                        dve.wait_ge(S["rdeg_ready"], GROUPS)
                    nc.vector.scalar_tensor_tensor(
                        out=zn[:, k * D:(k + 1) * D], in0=fin[:, (t % 2) * 512:(t % 2) * 512 + D],
                        scalar=rdeg[:, g * TPG + k:g * TPG + k + 1], in1=selfb[t % 2],
                        op0=ALU.mult, op1=ALU.add).then_inc(S["v_ready"], 1)
                    dve.wait_ge(S["v_ready"], t + 1)
                    dve.wait_ge(S["x1f_ready"], t + 1)
                    nc.vector.scalar_tensor_tensor(
                        out=zn[:, k * D:(k + 1) * D], in0=zn[:, k * D:(k + 1) * D], scalar=0.0,
                        in1=x1f[n % 2][:, k * D:(k + 1) * D], op0=ALU.max, op1=ALU.add
                    ).then_inc(S["z_ready"], 1)
                    halves(zn[:, k * D:(k + 1) * D], k, S["z_ready"], t + 1, S["st2_ready"])
                dve.wait_ge(S["st2_ready"], t + 1)
                moments(tiles, S["mv2_ready"])

            calls = [0]

            def layer1_norm(n, tiles):
                zn = z[n % 2]
                inv_std(calls[0], 1.0, EPS * SCALE * SCALE, S["mv2_ready"], n * TPG + tiles[-1] + 1,
                        S["r2_steps"], S["rstd2_ready"])
                calls[0] += 1
                dve.wait_ge(S["rstd2_ready"], calls[0])
                for k in tiles:
                    nc.vector.tensor_scalar(zn[:, k * D:(k + 1) * D], zn[:, k * D:(k + 1) * D],
                                            mv[:, 2 * k:2 * k + 1], rstd[:, k:k + 1], ALU.subtract, ALU.mult
                                            ).then_inc(S["out_ready"], 1)

            gather(0)
            gather(1)
            for n in range(GROUPS - 1):
                layer1(n, range(TPG))
                for m in range(3, GROUPS - 1):
                    if SUM_STEPS[m][-1] == n:
                        gather(m)
                layer1_norm(n, range(TPG))
            for pair in ((0, 1), (2, 3)):
                layer1(GROUPS - 1, pair)
                layer1_norm(GROUPS - 1, pair)

        @block.tensor
        def _(pe):
            mm = nc.tensor.matmul

            def fold(dst, lhs, rhs0):
                for h in range(DH):
                    for m in range(DH):
                        last = mm(dst[:, h * D:(h + 1) * D], lhs[:, m * D + h * P:m * D + (h + 1) * P],
                                  wc_r[:, (rhs0 + m) * D:(rhs0 + m + 1) * D], start=(m == 0), stop=(m == DH - 1))
                last.then_inc(S["wprod_ready"], 1)

            pe.wait_ge(S["ones_set"], 2)
            pe.wait_ge(S["wn_in"], 16)
            for m in range(DH):
                last = mm(acc0[:, 0:D], ones_r, wn_r[:, m * D:(m + 1) * D], start=(m == 0), stop=(m == DH - 1))
            last.then_inc(S["wprod_ready"], 1)

            def folds():
                pe.wait_ge(S["raw_in"], 64)
                pe.wait_ge(S["comb_taken"], 1)
                fold(work[:, 0:512], ws_r, 0)
                fold(work[:, 512:1024], wb_r, DH)
                for m in range(2 * DH):
                    last = mm(acc1[0:3, 0:D], bc_r[:, 3 * m:3 * m + 3], wc_r[:, m * D:(m + 1) * D],
                              start=(m == 0), stop=(m == 2 * DH - 1))
                last.then_inc(S["wprod_ready"], 1)

            def layer0_products(g, tiles):
                if tiles[0] == 2:
                    pe.wait_ge(S["x0T_in"], 16 * (g + 1))
                    if g == 0:
                        pe.wait_ge(S["w0_in"], 16)
                    else:
                        pe.wait_ge(S["pre_ready"], TPG * g - 2)
                bank = psX if tiles[0] == 2 else psS
                for k in tiles:
                    for h in range(DH):
                        last = mm(bank[:, k % 2 * D:(k % 2 + 1) * D], x0T[:, h * IW + k * P:h * IW + (k + 1) * P],
                                  w0[:, h * D:(h + 1) * D], start=(h == 0), stop=(h == DH - 1))
                last.then_inc(S["l0_ready"], 1)

            def neighbour_sums(g, first, end):
                if g == 0 and first == 0:
                    pe.wait_ge(S["xs_ready"], 2)
                elif first == 0:
                    pe.wait_ge(S["pre_ready"], TPG * g)
                for j in range(first, end):
                    if j % CT == 0:
                        pe.wait_ge(S["mask_ready"], g * CHUNKS + j // CT + 1)
                    q = j % 4 * SREP
                    last = mm(psS[q:q + SREP, :], xs[:, j * SREP:(j + 1) * SREP],
                              mask8[:, (g * JT + j) * IW:(g * JT + j + 1) * IW],
                              start=(j < 4), stop=(j >= JT - 4), tile_position=(0, q))
                if end == JT:
                    last.then_inc(S["s_ready"], 1)

            def columns(g):
                pe.wait_ge(S["srow_ready"], g + 1)
                if g == 0:
                    pe.wait_ge(S["comb_in"], 16)
                elif g == 1:
                    pe.wait_ge(S["wprod_taken"], 3)
                elif g >= 3:
                    pe.wait_ge(S["part_ready"], g - 2)
                for k in range(TPG):
                    last = mm(work[:, 2 * k:2 * k + 2], srow[:, k * P:(k + 1) * P], comb[:, :],
                              start=True, stop=True)
                last.then_inc(S["comb_ready"], 1)

            def aggregate(dst, g, j, start, stop):
                for part in range(2):
                    for h in range(DH):
                        o = (j * 2 + part) * D + h * P
                        last = mm(dst[:, h * IW:(h + 1) * IW], x1hl[:, o:o + P],
                                  mask8[:, (g * JT + j) * IW:(g * JT + j + 1) * IW],
                                  start=(start and part == 0), stop=(stop and part == 1))
                return last

            def open_sum(h, g, tiles):
                for k in tiles:
                    pe.wait_ge(S["lo_ready"], TPG * g + k + 1)
                    if h == 0 and g == 0 and k == 0:
                        pe.wait_ge(S["wprod_taken"], 1)
                    j = TPG * g + k
                    last = aggregate((acc0, acc1)[h], h, j, j == 0, j == JT - 1)
                if j == JT - 1:
                    last.then_inc(S[("acc0_ready", "acc1_ready")[h]], 1)

            neighbour_sums(0, 0, AHEAD * CT)
            for g in range(GROUPS):
                layer0_products(g, (2, 3))
                if g >= 1:
                    open_sum(0, g - 1, (0, 1))
                neighbour_sums(g, AHEAD * CT, JT)
                if g >= 1:
                    open_sum(0, g - 1, (2, 3))
                columns(g)
                layer0_products(g, (0, 1))
                if g == 0:
                    folds()
                elif g == 1:
                    pe.wait_ge(S["bsum_ready"], 1)
                else:
                    pe.wait_ge(S["comb_taken"], g + 1)
                dst = acc1 if g == 1 else work
                for j in range(TPG * g):
                    aggregate(dst, g, j, j == 0, False)
                if g + 1 < GROUPS:
                    neighbour_sums(g + 1, 0, AHEAD * CT)
                if g >= 1:
                    for k in range(TPG):
                        pe.wait_ge(S["lo_ready"], TPG * g + k + 1)
                        last = aggregate(dst, g, TPG * g + k, False, g > 1 and k == TPG - 1)
                    if g >= 2:
                        last.then_inc(S["sum_ready"], 1)
                        open_sum(1, g, range(TPG))
            open_sum(0, GROUPS - 1, range(TPG))

            def turn_x1(n):
                for h in range(2):
                    bank = psS if h == 0 else psX
                    if n >= 1:
                        pe.wait_ge(S["x1T_ready"], 2 * (n - 1) + h + 1)
                    elif h == 1:
                        pe.wait_ge(S["pre_ready"], TPG * GROUPS)
                    pe.wait_ge(S["x1f_ready"], TPG * n + 2 * h + 2)
                    for q in range(4):
                        k, f = 2 * h + q // 2, q % 2
                        last = nc.tensor.transpose(bank[:, q * P:(q + 1) * P],
                                                   x1f[n % 2][:, k * D + f * P:k * D + (f + 1) * P], ident[:, :])
                    last.then_inc(S["xt_ready"], 1)

            def layer1_products(n, k):
                t = n * TPG + k
                b = (t % 2) * 512
                if k == 0 and n != 2:
                    pe.wait_ge(S["agg_ready"], n + 1 if n < 2 else n)
                if t == 0:
                    pe.wait_ge(S["bias_ready"], 1)
                if t < 2:
                    pe.wait_ge(S["whole1_ready"], 1)
                else:
                    pe.wait_ge(S["v_ready"], t - 1)
                agg = sums(FINAL_ORDER[n])
                for h in range(DH):
                    mm(fin[:, b:b + D], agg[:, h * IW + k * P:h * IW + (k + 1) * P],
                       wnb[:, h * D:(h + 1) * D], start=(h == 0), stop=(h == DH - 1))
                mm(fin[:, b + D:b + 2 * D], ones3[:, :], bias3[:, :], start=True, stop=False)
                if k % 2 == 0:
                    pe.wait_ge(S["x1T_ready"], 2 * n + k // 2 + 1)
                for h in range(DH):
                    last = mm(fin[:, b + D:b + 2 * D], x1T[:, (2 * k + h) * P:(2 * k + h + 1) * P],
                              wself[:, h * D:(h + 1) * D], start=False, stop=(h == DH - 1))
                last.then_inc(S["fin_ready"], 1)

            def sum_rest(m, tiles):
                g = FINAL_ORDER[m]
                for j in tiles:
                    last = aggregate(work if m % 2 else acc0, g, j, j == TPG * (g + 1), j == JT - 1)
                    if j == JT - 1:
                        last.then_inc(S["sum2_ready"], 1)

            pe.wait_ge(S["ident_in"], 16)
            for n in range(GROUPS):
                turn_x1(n)
                todo = [(m, j) for m in SUM_STEPS if n in SUM_STEPS[m] for j in share(m, n)]
                if n == SUM_STEPS.get(todo[0][0], [None])[0] if todo else False:
                    m = todo[0][0]
                    pe.wait_ge(S["agg_ready"], m - 2 if m > 3 else 1)
                parts = TPG - 1 if n == GROUPS - 2 else TPG
                for k in range(TPG):
                    for m, j in todo[len(todo) * k // parts:len(todo) * (k + 1) // parts]:
                        sum_rest(m, [j])
                    layer1_products(n, k)


FINAL_ORDER = [GROUPS - 1, 0, 1] + list(range(GROUPS - 2, 1, -1))
SUM_STEPS = {3: [0], 4: [1], 5: [2], 6: [3, 4], 7: [5, 6]}


def share(m, n):
    first = TPG * (FINAL_ORDER[m] + 1)
    steps = SUM_STEPS[m]
    i = steps.index(n)
    cut = [first + (JT - first) * q // len(steps) for q in range(len(steps) + 1)]
    return range(cut[i], cut[i + 1])


def kernel(**inputs):
    import numpy as _np
    import concourse.bacc as _bacc
    from concourse import mybir as _mybir
    from concourse.bass_utils import run_bass_kernel_spmd as _run

    a = {k: _np.asarray(v) for k, v in inputs.items()}
    x = a["x"]
    rows = lambda w, t: w.reshape(t, P, -1).transpose(1, 0, 2).reshape(P, -1)
    bias = _np.concatenate([a["L1_gnn_b_self"], a["L1_gnn_b_nb"]]).reshape(2 * DH, P)
    comb = _np.zeros((P, 2), _np.float32)
    for q in range(4):
        comb[q * SREP:q * SREP + 3, 0] = 1.0
        comb[q * SREP + 3, 1] = 1.0
    arrays = {
        "adjT": a["adj"].reshape(GROUPS, IW, CHUNKS, CT, P).transpose(0, 2, 4, 3, 1)
                        .reshape(GROUPS * CHUNKS, P, CT * IW),
        "xtile": x.reshape(GROUPS, TPG, P, D).transpose(0, 2, 1, 3).reshape(GROUPS, P, TPG * D),
        "xT": x.T.reshape(DH, P, GROUPS, IW).transpose(2, 1, 0, 3).reshape(GROUPS, P, DH * IW),
        "xcol": x[:, 0].reshape(JT, P).T,
        "w0T": rows(a["L0_gnn_w_self"].T, DH),
        "wnT": rows(a["L0_gnn_w_neigh"].T, DH),
        "wsT": rows(a["L1_gnn_W_self"].T, DH),
        "wbT": rows(a["L1_gnn_W_nb"].T, DH),
        "wc": rows(a["L1_gnn_W_comb"], 2 * DH),
        "bcol": _np.repeat(bias.T, 3, axis=1),
        "bcomb": _np.broadcast_to(a["L1_gnn_b_comb"], (3, D)),
        "ident": _np.eye(P, dtype=_np.float32),
        "comb": comb,
        "sel": _np.eye(3, dtype=_np.float32),
    }
    arrays = {k + "_dram": _np.ascontiguousarray(v) for k, v in arrays.items()}
    nc = _bacc.Bacc("TRN2", target_bir_lowering=False, num_devices=1)
    args = [nc.dram_tensor(k, v.shape, _mybir.dt.from_np(v.dtype), kind="ExternalInput").ap()
            for k, v in arrays.items()]
    out = nc.dram_tensor("out_dram", (GROUPS, P, TPG * D), F32, kind="ExternalOutput").ap()
    build(nc, *args, out)
    r = _run(nc, [arrays], core_ids=[0]).results[0]["out_dram"]
    return r.reshape(GROUPS, P, TPG, D).transpose(0, 2, 1, 3).reshape(N, D)
```

```python
from contextlib import ExitStack

import concourse.bass as bass
from concourse import mybir
from concourse.alu_op_type import AluOpType as ALU

ACT = mybir.ActivationFunctionType
F32 = mybir.dt.float32
F16 = mybir.dt.float16
BF16 = mybir.dt.bfloat16
FP8 = mybir.dt.float8e4
AX = mybir.AxisListType
I32 = mybir.dt.int32
U8 = mybir.dt.uint8

P = 128
N = 4096
D = 256
DH = D // P
IW = 512
GROUPS = N // IW
TPG = IW // P
JT = N // P
CT = 2
CHUNKS = JT // CT
SLOTS = 4
EARLY = 5
LEAD = EARLY - 1
TURN_BEHIND = {0: [2], 1: [3], 3: [4], 5: [5], 7: [6], 8: [7], 13: [8], 14: [9]}
PRODUCT_BEHIND = {1: [2], 3: [3], 5: [4], 7: [5], 10: [6], 12: [7]}
FOLD_GROUP = 1
RAW_AHEAD = 4
AHEAD = 6
RSQRT_SEED = float(0x5F1FFFF9)
RSQRT_GAIN, RSQRT_TERM = 0.703952253, 2.38924456
SCALE = 2.0 ** 11
EPS = 1e-5
SREP = 32
BN = 6
MANTISSA = 23
LAST_GATHER = 2
INV_STEPS = 11


def build(nc, adjT, xtile, xT, xcol, w0T, wnT, wsT, wbT, wc, bcol, bcomb, ident_d, comb_d, sel_d, out):
    with ExitStack() as ctx:
        def sb(name, shape, dt):
            return ctx.enter_context(nc.sbuf_tensor(name, shape, dt))

        def sem(name):
            return ctx.enter_context(nc.semaphore(name))

        mask = sb("mask", [P, GROUPS * JT * IW], U8)
        mask8 = mask[:, :].bitcast(FP8)
        part32 = mask[:, :].bitcast(F32)
        ROW32 = JT * IW // 4

        def sums(g):
            return part32[:, bass.ds(g * ROW32, DH * IW)]

        def columns_of(sum_, half):
            if half is None:
                return sum_
            return sum_.rearrange("p (h i) -> p h i", h=DH)[:, :, half * (IW // 2):(half + 1) * (IW // 2)]

        def sum_parts(g, part):
            o = g * ROW32 + DH * IW + part * DH * IW // 2
            return part32[:, o:o + DH * IW // 2].bitcast(F16)

        x1hl = sb("x1hl", [P, JT * 2 * D], F16)
        ARENA = 7168
        arena = sb("arena", [P, ARENA], F32)
        SLOTW = CT * IW
        stage = [arena[:, k * SLOTW:(k + 1) * SLOTW].bitcast(I32) for k in range(SLOTS)]
        GD = TPG * D
        x0 = arena[:, SLOTS * SLOTW:SLOTS * SLOTW + GD]
        x0T = arena[:, SLOTS * SLOTW + GD:SLOTS * SLOTW + 2 * GD]
        x1s = arena[:, SLOTS * SLOTW + 2 * GD:SLOTS * SLOTW + 3 * GD]
        x1f = [arena[:, k * GD:(k + 1) * GD] for k in range(2)]
        z = [arena[:, 2 * GD + k * GD:3 * GD + k * GD] for k in range(2)]
        x1T = [arena[:, (4 + k) * GD:(5 + k) * GD].bitcast(F16) for k in range(2)]
        selfb = [arena[:, 6 * GD + k * D:6 * GD + (k + 1) * D] for k in range(2)]
        X_EARLY = (GROUPS - 2) * ROW32 - GD
        x_early = [part32[:, X_EARLY + e * GD:X_EARLY + (e + 1) * GD] for e in range(EARLY)]
        l0_32 = x1hl[:, :].bitcast(F32)
        w0 = sb("w0", [P, DH * D], F32)
        wself_hi, wself_lo = (sb("wself_" + part, [P, DH * D], F16) for part in ("hi", "lo"))
        wnb_hi, wnb_lo, wnb_hi2 = (sb("wnb_" + part, [P, DH * D], F16) for part in ("hi", "lo", "hi2"))
        wmax = sb("wmax", [P, 2], F32)
        wexp = sb("wexp", [P, 2], I32)
        wscale = sb("wscale", [P, 2], F32)
        wunscale = sb("wunscale", [P, 2], F32)
        wnsum = sb("wnsum", [P, D], F32)
        bias3 = sb("bias3", [3, D], BF16)
        ones3 = sb("ones3", [3, P], BF16)
        ident = sb("ident", [P, P], F32)
        ident16 = sb("ident16", [P, P], F16)
        comb = sb("comb", [P, 2], F32)
        xs = sb("xs", [P, JT * SREP], BF16)
        xc = sb("xc", [P, JT], F32)
        srow = sb("srow", [P, IW], F32)
        sdeg = sb("sdeg", [P, 2 * TPG], F32)
        scol = sb("scol", [P, TPG], F32)
        dmax = sb("dmax", [P, TPG], F32)
        rdeg = sb("rdeg", [P, JT], F32)
        nb_scale = sb("nb_scale", [P, JT], F32)
        stats = sb("stats", [P, TPG * BN], F32)
        mv = sb("mv", [P, TPG * 2], F32)
        ve = sb("ve", [P, TPG], F32)
        sd = sb("sd", [P, TPG], F32)
        r0 = sb("r0", [P, TPG], F32)
        r1 = sb("r1", [P, TPG], F32)
        rt = sb("rt", [P, TPG], F32)
        mv2 = [sb("mv2_%d" % b, [P, TPG * 2], F32) for b in range(2)]
        rstd2 = [sb("rstd2_%d" % b, [P, TPG], F32) for b in range(2)]
        shift = [sb("shift%d" % b, [P, TPG], F32) for b in range(2)]
        pve, pr, pu, pr2 = (sb(n, [P, TPG], F32) for n in ("pve", "pr", "pu", "pr2"))
        rstd = sb("rstd", [P, TPG], F32)
        raw = part32[:, (GROUPS - 1) * ROW32:]
        raw_at = [0]

        def in_raw(parts, words):
            start, raw_at[0] = raw_at[0], raw_at[0] + words
            return raw[0:parts, start:start + words]

        wn_r, ws_r, wb_r = (in_raw(P, DH * D) for _ in range(3))
        wc_r = in_raw(P, 2 * DH * D)
        bc_r = in_raw(P, 3 * 2 * DH)
        ones_r = in_raw(P, P)
        bcomb_r, bsum, brem, bacc = (in_raw(3, D) for _ in range(4))
        bpart = in_raw(3, D // 2).bitcast(BF16)
        sel = in_raw(3, 3)
        wself, wnb = wn_r, ws_r

        def ps(name, banks):
            return ctx.enter_context(nc.psum_tensor(name, [P, banks * 512], F32))
        acc0 = ps("acc0", 2)
        acc1 = ps("acc1", 2)
        work = ps("work", 2)
        psS = ps("psS", 1)
        psX = ps("psX", 1)
        fin = acc1

        names = """w0_in comb_in bias_steps bsum_ready xc_in wn_in ident_in b_in raw_in adj0 adj1 adj2 adj3 x0_in
            x0T_in ones_set xs_ready wprod_ready wprod_taken bias_ready mask_ready l0_ready
            s_ready srow_ready comb_ready comb_taken scol_ready rdeg_ready pre_ready u_ready
            st_ready mv_ready r_steps rstd_ready x1s_ready hi_ready lo_ready sum_ready
            part_ready acc0_ready x1f_ready xt_ready x1T_ready agg_ready sum2_ready fin_ready
            selfb_ready v_ready z_ready st2_ready mv2_ready r2_steps rstd2_ready out_ready
            acc1_ready whole1_ready out_done0 out_done1 prep dmax_ready wmax_ready wsum_ready
            wscale_steps wscale_ready wparts_ready ident16_ready agg_hi agg_lo nb_scale_ready
            turned xT_taken l0_taken shift_ready pool_steps last_shift act_out""".split()
        S = {n: sem(n) for n in names}
        adj_in = [S["adj%d" % k] for k in range(SLOTS)]
        x_early_in = [sem("x_early_in%d" % e) for e in range(EARLY)]
        out_done = [S["out_done%d" % k] for k in range(2)]

        block = ctx.enter_context(nc.Block())

        @block.sync
        def _(sp):
            def load(chunk, slot):
                sp.dma_start(stage[slot], adjT[bass.ds(chunk, 1), :, :].rearrange("c p n -> p (c n)")
                             ).then_inc(adj_in[slot], 16)

            load(0, 0)
            sp.dma_start(x_early[0], xtile[0]).then_inc(x_early_in[0], 16)
            sp.dma_start(ident[:, :], ident_d).then_inc(S["ident_in"], 16)
            sp.dma_start(w0[:, :], w0T).then_inc(S["w0_in"], 16)
            for s in range(1, SLOTS):
                load(s, s)
            with sp.Fori(1, GROUPS * CHUNKS // SLOTS) as m:
                for s in range(SLOTS):
                    sp.wait_ge(S["mask_ready"], m * SLOTS + (s + 1 - SLOTS))
                    load(m * SLOTS + s, s)
            for n, g in enumerate(FINAL_ORDER):
                for h in range(2):
                    if n < GROUPS - 1:
                        sp.wait_ge(S["act_out"], TPG * n + 2 * h + 2)
                    elif h == 0:
                        sp.wait_ge(S["out_ready"], 2)
                    else:
                        sp.wait_ge(S["act_out"], TPG * n + 2)
                    sp.dma_start(out[g][:, h * 2 * D:(h + 1) * 2 * D], z[n % 2][:, h * 2 * D:(h + 1) * 2 * D]
                                 ).then_inc(out_done[n % 2], 16)
            for b in range(2):
                sp.wait_ge(out_done[b], 32 * (GROUPS // 2))

        @block.gpsimd
        def _(pool):
            pool.dma_start(xc[:, :], xcol).then_inc(S["xc_in"], 16)
            pool.dma_start(x_early[1], xtile[1]).then_inc(x_early_in[1], 16)
            pool.dma_start(wn_r, wnT).then_inc(S["wn_in"], 16)
            pool.dma_start(x_early[2], xtile[2]).then_inc(x_early_in[2], 16)
            pool.dma_start(comb[:, :], comb_d).then_inc(S["comb_in"], 16)
            for e in range(3, EARLY):
                pool.dma_start(x_early[e], xtile[e]).then_inc(x_early_in[e], 16)

            def next_xT(g):
                pool.wait_ge(S["l0_ready"], 2 * g)
                pool.dma_start(x0T, xT[g]).then_inc(S["x0T_in"], 16)

            def next_x(g):
                pool.wait_ge(S["x1s_ready"], TPG * g)
                pool.dma_start(x0, xtile[g]).then_inc(S["x0_in"], 16)

            next_xT(EARLY)
            pool.wait_ge(S["mask_ready"], (FOLD_GROUP + 1) * CHUNKS - RAW_AHEAD)
            for dst, src in ((ws_r, wsT), (wb_r, wbT), (wc_r, wc), (bc_r, bcol)):
                pool.dma_start(dst, src).then_inc(S["raw_in"], 16)
            pool.dma_start(bcomb_r, bcomb).then_inc(S["b_in"], 16)
            pool.dma_start(sel, sel_d).then_inc(S["b_in"], 16)
            next_xT(EARLY + 1)

            steps = [0]

            def step(ins):
                steps[0] += 1
                ins.then_inc(S["bias_steps"], 1)
                pool.wait_ge(S["bias_steps"], steps[0])

            pool.wait_ge(S["b_in"], 32)
            pool.wait_ge(S["bsum_ready"], 1)
            step(nc.gpsimd.tensor_tensor(brem, bsum, bcomb_r, ALU.add))
            pool.wait_ge(S["wscale_ready"], 1)
            step(nc.gpsimd.tensor_scalar(brem, brem, wscale[0:3, 0:1], SCALE, ALU.mult, ALU.mult))
            step(nc.gpsimd.tensor_copy(bpart, brem))
            step(nc.gpsimd.tensor_scalar(bacc, bpart, sel[:, 0:1], None, ALU.mult))
            for m in range(1, 3):
                step(nc.gpsimd.tensor_tensor(brem, brem, bpart, ALU.subtract))
                step(nc.gpsimd.tensor_copy(bpart, brem))
                step(nc.gpsimd.tensor_scalar(bsum, bpart, sel[:, m:m + 1], None, ALU.mult))
                step(nc.gpsimd.tensor_tensor(bacc, bacc, bsum, ALU.add))
            nc.gpsimd.tensor_copy(bias3[:, :], bacc).then_inc(S["bias_ready"], 1)

            next_xT(EARLY + 2)
            for g in range(EARLY, GROUPS):
                next_x(g)

            def x1_float32(n):
                if n == 0:
                    pool.wait_ge(S["lo_ready"], JT)
                if n >= 2:
                    pool.wait_ge(S["z_ready"], TPG * (n - 1))
                for k in range(TPG):
                    o = (FINAL_ORDER[n] * TPG + k) * 2 * D
                    nc.gpsimd.tensor_tensor(x1f[n % 2][:, k * D:(k + 1) * D], x1hl[:, o:o + D],
                                            x1hl[:, o + D:o + 2 * D], ALU.add).then_inc(S["x1f_ready"], 1)

            taken = [0]

            def link(ins):
                taken[0] += 1
                ins.then_inc(S["pool_steps"], 1)
                pool.wait_ge(S["pool_steps"], taken[0])

            def scale_and_shift(n):
                moments = mv2[n % 2][:, :].rearrange("p (k c) -> p c k", c=2)
                scale = rstd2[n % 2]
                tt, ts = nc.gpsimd.tensor_tensor, nc.gpsimd.tensor_scalar
                pool.wait_ge(S["mv2_ready"], TPG * (n + 1))
                if n >= 2:
                    pool.wait_ge(S["act_out"], TPG * (n - 1))
                link(ts(pve[:, :], moments[:, 1, :], EPS * SCALE * SCALE, None, ALU.add))
                link(ts(pr[:, :].bitcast(I32), pve[:, :].bitcast(I32), -0.5, RSQRT_SEED, ALU.mult, ALU.add))
                link(tt(pu[:, :], pr[:, :], pr[:, :], ALU.mult))
                link(tt(pu[:, :], pu[:, :], pve[:, :], ALU.mult))
                link(ts(pu[:, :], pu[:, :], -RSQRT_GAIN, RSQRT_GAIN * RSQRT_TERM, ALU.mult, ALU.add))
                link(tt(pr2[:, :], pr[:, :], pu[:, :], ALU.mult))
                link(tt(pu[:, :], pr2[:, :], pr2[:, :], ALU.mult))
                link(tt(pu[:, :], pu[:, :], pve[:, :], ALU.mult))
                link(ts(pve[:, :], pu[:, :], 3 / 8, -5 / 4, ALU.mult, ALU.add))
                link(tt(pve[:, :], pve[:, :], pu[:, :], ALU.mult))
                link(ts(pve[:, :], pve[:, :], 15 / 8, None, ALU.add))
                link(tt(scale[:, :], pr2[:, :], pve[:, :], ALU.mult))
                link(tt(pu[:, :], moments[:, 0, :], scale[:, :], ALU.mult))
                ts(shift[n % 2][:, :], pu[:, :], -1.0, None, ALU.mult).then_inc(S["shift_ready"], 1)

            x1_float32(0)
            x1_float32(1)
            for n in range(GROUPS - 1):
                scale_and_shift(n)
                if n + 2 < GROUPS:
                    x1_float32(n + 2)

        @block.scalar
        def _(act):
            for g in range(GROUPS):
                if g == GROUPS - 3:
                    act.wait_ge(S["u_ready"], TPG)
                if g == GROUPS - 2:
                    act.wait_ge(S["u_ready"], TPG * EARLY)
                if g == GROUPS - 1:
                    act.wait_ge(S["bias_ready"], 1)
                for c in range(CHUNKS):
                    act.wait_ge(adj_in[c % SLOTS], 16 * (g * CHUNKS // SLOTS + c // SLOTS + 1))
                    o = (g * JT + c * CT) * IW
                    nc.scalar.activation(mask8[:, o:o + CT * IW], stage[c % SLOTS], ACT.Sign, saturate=False
                                         ).then_inc(S["mask_ready"], 1)

            def transposed(n):
                for h in range(2):
                    act.wait_ge(S["xt_ready"], 2 * n + h + 1)
                    if n >= 2 and h == 0:
                        act.wait_ge(S["fin_ready"], TPG * (n - 1))
                    if n == 0 and h == 0:
                        act.wait_ge(S["lo_ready"], JT)
                    bank = (psS if h == 0 else psX)[:, :].bitcast(F16)
                    nc.scalar.copy(x1T[n % 2][:, h * 1024:(h + 1) * 1024], bank).then_inc(S["x1T_ready"], 1)

            def sum_high(n, half=None):
                g = FINAL_ORDER[n]
                if n == 2:
                    act.wait_ge(S["whole1_ready"], 1)
                else:
                    act.wait_ge(S["agg_ready"], n + 1 if n < 2 else n + (half or 0))
                nc.scalar.activation(columns_of(sum_parts(g, 0), half), columns_of(sums(g), half), ACT.Copy,
                                     scale=2.0 ** -11).then_inc(S["agg_hi"], 1)

            def act_norm(n, tiles):
                if n < GROUPS - 1:
                    act.wait_ge(S["shift_ready"], n + 1)
                else:
                    act.wait_ge(S["last_shift"], 1)
                for k in tiles:
                    nc.scalar.activation(z[n % 2][:, k * D:(k + 1) * D], z[n % 2][:, k * D:(k + 1) * D],
                                         ACT.Identity, bias=shift[n % 2][:, k:k + 1], scale=rstd2[n % 2][:, k:k + 1]
                                         ).then_inc(S["act_out"], 1)

            def self_parts(n, tiles):
                for k in tiles:
                    t = n * TPG + k
                    act.wait_ge(S["fin_ready"], t + 1)
                    if t >= 2:
                        act.wait_ge(S["v_ready"], t - 1)
                    nc.scalar.activation(selfb[t % 2], fin[:, (t % 2) * 512 + D:(t % 2) * 512 + 2 * D],
                                         ACT.Copy, scale=wunscale[:, 0:1]).then_inc(S["selfb_ready"], 1)

            sum_high(0)
            act.wait_ge(S["acc1_ready"], 1)
            nc.scalar.activation(sums(1), acc1[:, :], ACT.Copy, scale=0.5).then_inc(S["whole1_ready"], 1)
            for n in range(GROUPS - 1):
                if n == 0:
                    transposed(0)
                    sum_high(1)
                    sum_high(2)
                if n < GROUPS - 2:
                    self_parts(n, (0, 1))
                    if n >= 1:
                        act_norm(n - 1, range(TPG))
                    transposed(n + 1)
                    self_parts(n, (2, 3))
                    for m in range(3, GROUPS - 1):
                        if SUM_STEPS[m][-1] == n:
                            sum_high(m)
                else:
                    act_norm(n - 1, range(TPG))
                    self_parts(n, (0,))
                    for half in range(2):
                        sum_high(n + 1, half)
                    self_parts(n, (1, 2))
                    transposed(n + 1)
                    self_parts(n, (3,))
            self_parts(GROUPS - 1, range(TPG))
            act_norm(GROUPS - 2, range(TPG))
            act_norm(GROUPS - 1, (2, 3))

        @block.vector
        def _(dve):
            nc.vector.memset(xs[:, :], 0.0).then_inc(S["prep"], 1)
            nc.vector.memset(ones3[:, :], 1.0).then_inc(S["ones_set"], 1)
            nc.vector.memset(ones_r, 1.0).then_inc(S["ones_set"], 1)
            xsv = xs[:, :].rearrange("p (j c) -> p c j", c=SREP)
            dve.wait_ge(S["xc_in"], 16)
            dve.wait_ge(S["prep"], 1)
            nc.vector.tensor_copy(xsv[:, 0, :], xc[:, :]).then_inc(S["prep"], 1)
            dve.wait_ge(S["prep"], 2)
            nc.vector.tensor_tensor(xc[:, :], xc[:, :], xsv[:, 0, :], ALU.subtract).then_inc(S["prep"], 1)
            dve.wait_ge(S["prep"], 3)
            nc.vector.tensor_copy(xsv[:, 1, :], xc[:, :]).then_inc(S["prep"], 1)
            dve.wait_ge(S["prep"], 4)
            nc.vector.tensor_tensor(xc[:, :], xc[:, :], xsv[:, 1, :], ALU.subtract).then_inc(S["prep"], 1)
            dve.wait_ge(S["prep"], 5)
            nc.vector.tensor_copy(xsv[:, 2, :], xc[:, :]).then_inc(S["xs_ready"], 1)
            nc.vector.memset(xsv[:, 3, :], 1.0).then_inc(S["xs_ready"], 1)

            dve.wait_ge(S["ident_in"], 16)
            nc.vector.tensor_copy(ident16[:, :], ident[:, :]).then_inc(S["ident16_ready"], 1)

            def take_xT(n):
                dve.wait_ge(S["turned"], n + 1)
                if n >= 2:
                    dve.wait_ge(S["l0_ready"], n - 1)
                half = n % 2
                nc.vector.tensor_copy(x0T.rearrange("p (h i) -> p h i", h=DH)[:, :, half * 2 * P:(half + 1) * 2 * P],
                                      work[:, half * 512:(half + 1) * 512].rearrange("p (h i) -> p h i", h=DH)
                                      ).then_inc(S["xT_taken"], 1)

            def take_l0(g, half, bank):
                dve.wait_ge(S["l0_ready"], 2 * g + (half + 1))
                nc.vector.tensor_copy(l0_32[:, bass.ds(g * GD + half * 2 * D, 2 * D)], bank).then_inc(S["l0_taken"], 1)

            take_xT(0)
            take_xT(1)
            take_l0(0, 0, psX[:, :])
            take_l0(0, 1, acc1[:, 0:2 * D])
            dve.wait_ge(S["wprod_ready"], 1)
            nc.vector.tensor_copy(wnsum[:, :], acc0[:, 0:D]).then_inc(S["wprod_taken"], 1)
            for e in range(1, EARLY):
                take_xT(2 * e)
                take_xT(2 * e + 1)
                if e < LEAD:
                    take_l0(e, 0, psX[:, :])
                    take_l0(e, 1, acc1[:, 0:2 * D])

            def degrees(g):
                dve.wait_ge(S["s_ready"], g + 1)
                nc.vector.tensor_copy(srow[:, :], psS[:, :]).then_inc(S["srow_ready"], 1)
                dve.wait_ge(S["comb_ready"], g + 1)
                nc.vector.tensor_copy(sdeg[:, :], work[:, 0:2 * TPG]).then_inc(S["comb_taken"], 1)
                dve.wait_ge(S["comb_taken"], g + 1)
                sv = sdeg[:, :].rearrange("p (k c) -> p c k", c=2)
                nc.vector.scalar_tensor_tensor(out=scol[:, :], in0=sv[:, 1, :], scalar=0.0, in1=sv[:, 0, :],
                                               op0=ALU.is_gt, op1=ALU.mult).then_inc(S["scol_ready"], 1)
                nc.vector.tensor_scalar(dmax[:, :], sv[:, 1, :], 1.0, None, ALU.max).then_inc(S["dmax_ready"], 1)

            def pre_act(g, k):
                if k == 0:
                    dve.wait_ge(S["scol_ready"], g + 1)
                    dve.wait_ge(S["l0_taken"], 2 * g + 2)
                nc.vector.scalar_tensor_tensor(out=x1s[:, k * D:(k + 1) * D], in0=wnsum[:, :],
                                               scalar=scol[:, k:k + 1],
                                               in1=l0_32[:, bass.ds(g * GD + k * D, D)],
                                               op0=ALU.mult, op1=ALU.add).then_inc(S["pre_ready"], 1)

            def residual(g, x, k):
                if k == 0 and x is x0:
                    dve.wait_ge(S["x0_in"], g * 16 + (16 - 16 * EARLY))
                dve.wait_ge(S["pre_ready"], g * TPG + k + 1)
                nc.vector.scalar_tensor_tensor(out=x0[:, k * D:(k + 1) * D], in0=x1s[:, k * D:(k + 1) * D],
                                               scalar=0.0, in1=x[:, k * D:(k + 1) * D],
                                               op0=ALU.max, op1=ALU.add).then_inc(S["u_ready"], 1)

            def halves(src, k, value, count, done):
                dve.wait_ge(value, count)
                nc.vector.bn_stats(stats[:, k * BN:(k + 1) * BN], src).then_inc(done, 1)

            def moments(mv, tiles, last):
                for k in tiles:
                    nc.vector.bn_aggr(mv[:, 2 * k:2 * k + 2], stats[:, k * BN:(k + 1) * BN]).then_inc(last, 1)

            def inv_std(call, mv, rstd, gain, eps, moments_done, count, steps, done):
                at = call * INV_STEPS
                var = mv[:, :].rearrange("p (k c) -> p c k", c=2)[:, 1, :]
                dve.wait_ge(moments_done, count)
                nc.vector.tensor_scalar(ve[:, :], var, eps, None, ALU.add).then_inc(steps, 1)
                dve.wait_ge(steps, at + 1)
                nc.vector.tensor_scalar(r0[:, :].bitcast(I32), ve[:, :].bitcast(I32), -0.5, RSQRT_SEED,
                                        ALU.mult, ALU.add).then_inc(steps, 1)
                nc.vector.tensor_scalar(sd[:, :], ve[:, :], -0.5, None, ALU.mult).then_inc(steps, 1)
                for m, (r, scaled, factor) in enumerate(((r0, r1, 2 * RSQRT_GAIN), (r1, rstd, 1.5 * gain))):
                    at_m = at + 3 + 4 * m
                    dve.wait_ge(steps, at_m)
                    nc.vector.tensor_tensor(rt[:, :], r[:, :], r[:, :], ALU.mult).then_inc(steps, 1)
                    nc.vector.tensor_scalar(scaled[:, :], r[:, :], factor, None, ALU.mult).then_inc(steps, 1)
                    dve.wait_ge(steps, at_m + 1)
                    nc.vector.tensor_tensor(rt[:, :], rt[:, :], sd[:, :], ALU.mult).then_inc(steps, 1)
                    dve.wait_ge(steps, at_m + 3)
                    if m == 0:
                        nc.vector.scalar_tensor_tensor(out=r1[:, :], in0=rt[:, :], scalar=RSQRT_TERM / 2,
                                                       in1=r1[:, :], op0=ALU.add, op1=ALU.mult).then_inc(steps, 1)
                nc.vector.scalar_tensor_tensor(out=rt[:, :], in0=rt[:, :], scalar=5 / 3, in1=rt[:, :],
                                               op0=ALU.add, op1=ALU.mult).then_inc(steps, 1)
                dve.wait_ge(steps, at + INV_STEPS)
                nc.vector.scalar_tensor_tensor(out=rstd[:, :], in0=rt[:, :], scalar=5 / 4, in1=rstd[:, :],
                                               op0=ALU.add, op1=ALU.mult).then_inc(done, 1)

            def high(g, k):
                dve.wait_ge(S["x1s_ready"], g * TPG + k + 1)
                nc.vector.tensor_copy(x1hl[:, bass.ds((g * TPG + k) * 2 * D, D)],
                                      x1s[:, k * D:(k + 1) * D]).then_inc(S["hi_ready"], 1)

            def low(g, k):
                dve.wait_ge(S["hi_ready"], g * TPG + k + 1)
                o = (g * TPG + k) * 2 * D
                nc.vector.tensor_tensor(x1hl[:, bass.ds(o + D, D)], x1s[:, k * D:(k + 1) * D],
                                        x1hl[:, bass.ds(o, D)], ALU.subtract).then_inc(S["lo_ready"], 1)

            def normalise(k):
                nc.vector.tensor_scalar(x1s[:, k * D:(k + 1) * D], x0[:, k * D:(k + 1) * D],
                                        mv[:, 2 * k:2 * k + 1], rstd[:, k:k + 1], ALU.subtract, ALU.mult
                                        ).then_inc(S["x1s_ready"], 1)

            def group(g, x, ahead):
                if ahead:
                    take_l0(g + LEAD, 0, psX[:, :])
                    take_l0(g + LEAD, 1, psX[:, :])
                degrees(g)
                for k in range(TPG):
                    pre_act(g, k)
                for k in range(TPG):
                    residual(g, x, k)
                for k in range(TPG):
                    halves(x0[:, k * D:(k + 1) * D], k, S["u_ready"], g * TPG + k + 1, S["st_ready"])
                dve.wait_ge(S["dmax_ready"], g + 1)
                dve.wait_ge(S["st_ready"], g * TPG + TPG)
                nc.vector.reciprocal(rdeg[:, bass.ds(g * TPG, TPG)], dmax[:, :]).then_inc(S["rdeg_ready"], 1)
                moments(mv, range(TPG), S["mv_ready"])
                inv_std(g, mv, rstd, SCALE, EPS, S["mv_ready"], g * TPG + TPG, S["r_steps"], S["rstd_ready"])
                dve.wait_ge(S["rstd_ready"], g + 1)
                for k in range(TPG + 2):
                    if k < TPG:
                        normalise(k)
                    if 1 <= k < TPG + 1:
                        high(g, k - 1)
                    if k >= 2:
                        low(g, k - 2)

            def partial(g):
                dve.wait_ge(S["sum_ready"], g - 1)
                nc.vector.tensor_scalar(sums(g), work[:, :], 0.5, None, ALU.mult).then_inc(S["part_ready"], 1)

            def split_weights():
                dve.wait_ge(S["wprod_taken"], 3)
                for c, w in enumerate((wself, wnb)):
                    nc.vector.tensor_reduce(wmax[:, c:c + 1], w, AX.X, ALU.max,
                                            apply_absolute_value=True).then_inc(S["wmax_ready"], 1)
                dve.wait_ge(S["wsum_ready"], 1)
                nc.vector.tensor_scalar(wmax[:, :], work[:, 512:514], 2.0 ** -100, None, ALU.max
                                        ).then_inc(S["wscale_steps"], 1)
                dve.wait_ge(S["wscale_steps"], 1)
                nc.vector.tensor_scalar(wexp[:, :], wmax[:, :].bitcast(I32), MANTISSA, None,
                                        ALU.arith_shift_right).then_inc(S["wscale_steps"], 1)
                dve.wait_ge(S["wscale_steps"], 2)
                nc.vector.tensor_scalar(wscale[:, :].bitcast(I32), wexp[:, :], -2.0 ** MANTISSA,
                                        (14 + 2 * 127) * 2.0 ** MANTISSA, ALU.mult, ALU.add
                                        ).then_inc(S["wscale_ready"], 1)
                nc.vector.tensor_scalar(wunscale[:, :].bitcast(I32), wexp[:, :], 2.0 ** MANTISSA,
                                        -14 * 2.0 ** MANTISSA, ALU.mult, ALU.add).then_inc(S["wscale_steps"], 1)
                dve.wait_ge(S["wscale_ready"], 1)
                for c, (w, hi) in enumerate(((wself, wself_hi), (wnb, wnb_hi))):
                    nc.vector.tensor_scalar(hi[:, :], w, wscale[:, c:c + 1], None, ALU.mult
                                            ).then_inc(S["wscale_steps"], 1)
                dve.wait_ge(S["wscale_steps"], 5)
                for c, (w, hi, lo) in enumerate(((wself, wself_hi, wself_lo), (wnb, wnb_hi, wnb_lo))):
                    nc.vector.scalar_tensor_tensor(out=lo[:, :], in0=w, scalar=wscale[:, c:c + 1], in1=hi[:, :],
                                                   op0=ALU.mult, op1=ALU.subtract).then_inc(S["wparts_ready"], 1)
                nc.vector.tensor_scalar(wnb_hi2[:, :], wnb_hi[:, :], 2.0 ** -11, None, ALU.mult
                                        ).then_inc(S["wparts_ready"], 1)

            group(0, x_early[0], False)
            take_l0(LEAD, 0, psX[:, :])
            take_l0(LEAD, 1, acc1[:, 0:2 * D])
            group(FOLD_GROUP, x_early[1], True)
            dve.wait_ge(S["wprod_ready"], 2)
            nc.vector.tensor_copy(wself, work[:, 0:512]).then_inc(S["wprod_taken"], 1)
            dve.wait_ge(S["wprod_ready"], 3)
            nc.vector.tensor_copy(wnb, work[:, 512:1024]).then_inc(S["wprod_taken"], 1)
            dve.wait_ge(S["wprod_ready"], 4)
            nc.vector.tensor_copy(bsum, work[0:3, 0:D]).then_inc(S["bsum_ready"], 1)
            split_weights()
            with dve.Fori(2, LEAD) as g:
                group(g, part32[:, bass.ds(g * GD + X_EARLY, GD)], True)
                partial(g)
            group(LEAD, x_early[LEAD], False)
            partial(LEAD)
            with dve.Fori(EARLY, GROUPS - 1) as g:
                group(g, x0, False)
                partial(g)
            group(GROUPS - 1, x0, False)

            def gather(n, half=None):
                g = FINAL_ORDER[n]
                if n == 0:
                    dve.wait_ge(S["sum_ready"], g - 1)
                    nc.vector.tensor_scalar(sums(g), work[:, :], 0.5, None, ALU.mult).then_inc(S["agg_ready"], 1)
                elif n == 1:
                    dve.wait_ge(S["acc0_ready"], 1)
                    nc.vector.tensor_scalar(sums(g), acc0[:, :], 0.5, None, ALU.mult).then_inc(S["agg_ready"], 1)
                else:
                    dve.wait_ge(S["sum2_ready"], n - 2)
                    if n == 3:
                        dve.wait_ge(S["part_ready"], g - 1)
                    nc.vector.scalar_tensor_tensor(out=columns_of(sums(g), half),
                                                   in0=columns_of((work if n % 2 else acc0)[:, :], half), scalar=0.5,
                                                   in1=columns_of(sums(g), half), op0=ALU.mult, op1=ALU.add
                                                   ).then_inc(S["agg_ready"], 1)

            def sum_low(n, half=None):
                g = FINAL_ORDER[n]
                dve.wait_ge(S["agg_hi"], n + 1 + (half or 0))
                nc.vector.scalar_tensor_tensor(out=columns_of(sum_parts(g, 1), half),
                                               in0=columns_of(sum_parts(g, 0), half), scalar=-2.0 ** 11,
                                               in1=columns_of(sums(g), half), op0=ALU.mult, op1=ALU.add
                                               ).then_inc(S["agg_lo"], 1)

            def layer1(n, tiles):
                g, zn = FINAL_ORDER[n], z[n % 2]
                for k in tiles:
                    t = n * TPG + k
                    if k == 0 and n >= 2:
                        dve.wait_ge(out_done[n % 2], 32 * (n // 2))
                    if (n, k) == (GROUPS - 2, 1):
                        for half in range(2):
                            gather(n + 1, half)
                        for half in range(2):
                            sum_low(n + 1, half)
                    if k == TPG - 1:
                        if n >= 2:
                            dve.wait_ge(S["shift_ready"], n - 1)
                        dve.wait_ge(S["st2_ready"], t)
                        moments(mv2[n % 2], range(TPG - 1), S["mv2_ready"])
                    dve.wait_ge(S["selfb_ready"], t + 1)
                    if t == 0:
                        dve.wait_ge(S["nb_scale_ready"], 1)
                    nc.vector.scalar_tensor_tensor(
                        out=zn[:, k * D:(k + 1) * D], in0=fin[:, (t % 2) * 512:(t % 2) * 512 + D],
                        scalar=nb_scale[:, g * TPG + k:g * TPG + k + 1], in1=selfb[t % 2],
                        op0=ALU.mult, op1=ALU.add).then_inc(S["v_ready"], 1)
                    dve.wait_ge(S["v_ready"], t + 1)
                    dve.wait_ge(S["x1f_ready"], t + 1)
                    nc.vector.scalar_tensor_tensor(
                        out=zn[:, k * D:(k + 1) * D], in0=zn[:, k * D:(k + 1) * D], scalar=0.0,
                        in1=x1f[n % 2][:, k * D:(k + 1) * D], op0=ALU.max, op1=ALU.add
                    ).then_inc(S["z_ready"], 1)
                    halves(zn[:, k * D:(k + 1) * D], k, S["z_ready"], t + 1, S["st2_ready"])
                dve.wait_ge(S["st2_ready"], t + 1)
                moments(mv2[n % 2], range(TPG - 1, TPG), S["mv2_ready"])

            def last_norm():
                b = (GROUPS - 1) % 2
                zn, mv_, scale = z[b], mv2[b], rstd2[b]
                dve.wait_ge(S["act_out"], TPG * (GROUPS - 2))
                inv_std(0, mv_, scale, 1.0, EPS * SCALE * SCALE, S["mv2_ready"], JT, S["r2_steps"], S["rstd2_ready"])
                dve.wait_ge(S["rstd2_ready"], 1)
                mean = mv_[:, :].rearrange("p (k c) -> p c k", c=2)[:, 0, :]
                nc.vector.scalar_tensor_tensor(out=shift[b][:, :], in0=mean, scalar=-1.0, in1=scale[:, :],
                                               op0=ALU.mult, op1=ALU.mult).then_inc(S["last_shift"], 1)
                for k in range(2):
                    nc.vector.tensor_scalar(zn[:, k * D:(k + 1) * D], zn[:, k * D:(k + 1) * D],
                                            mv_[:, 2 * k:2 * k + 1], scale[:, k:k + 1], ALU.subtract, ALU.mult
                                            ).then_inc(S["out_ready"], 1)

            gather(0)
            dve.wait_ge(S["rdeg_ready"], GROUPS)
            nc.vector.tensor_scalar(nb_scale[:, :], rdeg[:, :], wunscale[:, 1:2], 2.0 ** 12, ALU.mult, ALU.mult
                                    ).then_inc(S["nb_scale_ready"], 1)
            sum_low(0)
            gather(1)
            sum_low(1)
            sum_low(2)
            for n in range(GROUPS):
                layer1(n, range(TPG))
                for m in range(3, GROUPS - 1):
                    if SUM_STEPS[m][-1] == n:
                        gather(m)
                        sum_low(m)
            last_norm()

        @block.tensor
        def _(pe):
            mm = nc.tensor.matmul

            def fold(dst, lhs, rhs0):
                for h in range(DH):
                    for m in range(DH):
                        last = mm(dst[:, h * D:(h + 1) * D], lhs[:, m * D + h * P:m * D + (h + 1) * P],
                                  wc_r[:, (rhs0 + m) * D:(rhs0 + m + 1) * D], start=(m == 0), stop=(m == DH - 1))
                last.then_inc(S["wprod_ready"], 1)

            def fold_weights():
                pe.wait_ge(S["raw_in"], 64)
                pe.wait_ge(S["comb_taken"], FOLD_GROUP + 1)
                fold(work[:, 0:512], ws_r, 0)
                fold(work[:, 512:1024], wb_r, DH)

            def sum_maxima():
                pe.wait_ge(S["wmax_ready"], 2)
                mm(work[:, 512:514], ones_r, wmax[:, :], start=True, stop=True).then_inc(S["wsum_ready"], 1)

            def fold_bias():
                pe.wait_ge(S["wprod_taken"], 2)
                for m in range(2 * DH):
                    last = mm(work[0:3, 0:D], bc_r[:, 3 * m:3 * m + 3], wc_r[:, m * D:(m + 1) * D],
                              start=(m == 0), stop=(m == 2 * DH - 1))
                last.then_inc(S["wprod_ready"], 1)

            def row_sums():
                pe.wait_ge(S["ones_set"], 2)
                pe.wait_ge(S["wn_in"], 16)
                for m in range(DH):
                    last = mm(acc0[:, 0:D], ones_r, wn_r[:, m * D:(m + 1) * D], start=(m == 0), stop=(m == DH - 1))
                last.then_inc(S["wprod_ready"], 1)

            def turn_x(n):
                g, half = n // 2, n % 2
                if n == 0:
                    pe.wait_ge(S["ident_in"], 16)
                if half == 0:
                    pe.wait_ge(x_early_in[g], 16)
                if n >= 2:
                    pe.wait_ge(S["xT_taken"], n - 1)
                for h in range(DH):
                    for k in range(2):
                        o = half * 512 + (2 * h + k) * P
                        last = nc.tensor.transpose(work[:, o:o + P], x_early[g][:, (2 * half + k) * D + h * P:
                                                                               (2 * half + k) * D + (h + 1) * P],
                                                   ident[:, :])
                last.then_inc(S["turned"], 1)

            def layer0_products(n):
                g, half = n // 2, n % 2
                early = g < EARLY
                if n == 0:
                    pe.wait_ge(S["w0_in"], 16)
                if early:
                    pe.wait_ge(S["xT_taken"], n + 1)
                elif half == 0:
                    pe.wait_ge(S["x0T_in"], 16 * (g - EARLY + 1))
                if n >= 2:
                    pe.wait_ge(S["l0_taken"], n - 1 if g <= LEAD else n)
                bank = acc1 if g <= LEAD and half else psX
                for k in range(2):
                    for h in range(DH):
                        o = h * IW + (2 * half + k) * P
                        last = mm(bank[:, k * D:(k + 1) * D], x0T[:, o:o + P],
                                  w0[:, h * D:(h + 1) * D], start=(h == 0), stop=(h == DH - 1))
                last.then_inc(S["l0_ready"], 1)

            def neighbour_sums(g, first, end):
                if g == 0 and first == 0:
                    pe.wait_ge(S["xs_ready"], 2)
                elif first == 0:
                    pe.wait_ge(S["srow_ready"], g)
                for j in range(first, end):
                    if j % CT == 0:
                        pe.wait_ge(S["mask_ready"], g * CHUNKS + j // CT + 1)
                    q = j % 4 * SREP
                    last = mm(psS[q:q + SREP, :], xs[:, j * SREP:(j + 1) * SREP],
                              mask8[:, (g * JT + j) * IW:(g * JT + j + 1) * IW],
                              start=(j < 4), stop=(j >= JT - 4), tile_position=(0, q))
                if end == JT:
                    last.then_inc(S["s_ready"], 1)

            def columns(g):
                pe.wait_ge(S["srow_ready"], g + 1)
                if g == 0:
                    pe.wait_ge(S["comb_in"], 16)
                elif g == FOLD_GROUP + 1:
                    pe.wait_ge(S["wscale_ready"], 1)
                elif g >= 3:
                    pe.wait_ge(S["part_ready"], g - 2)
                for k in range(TPG):
                    last = mm(work[:, 2 * k:2 * k + 2], srow[:, k * P:(k + 1) * P], comb[:, :],
                              start=True, stop=True)
                last.then_inc(S["comb_ready"], 1)

            def aggregate(dst, g, j, start, stop):
                for part in range(2):
                    for h in range(DH):
                        o = (j * 2 + part) * D + h * P
                        last = mm(dst[:, h * IW:(h + 1) * IW], x1hl[:, o:o + P],
                                  mask8[:, (g * JT + j) * IW:(g * JT + j + 1) * IW],
                                  start=(start and part == 0), stop=(stop and part == 1))
                return last

            def open_sum(h, g, tiles):
                last = None
                for k in tiles:
                    pe.wait_ge(S["lo_ready"], TPG * g + k + 1)
                    if h == 0 and g == 0 and k == 0:
                        pe.wait_ge(S["wprod_taken"], 1)
                    j = TPG * g + k
                    last = aggregate((acc0, acc1)[h], h, j, j == 0, j == JT - 1)
                if last is not None and j == JT - 1:
                    last.then_inc(S[("acc0_ready", "acc1_ready")[h]], 1)

            turn_x(0)
            turn_x(1)
            layer0_products(0)
            layer0_products(1)
            row_sums()
            for c in range(CHUNKS):
                neighbour_sums(0, c * CT, (c + 1) * CT)
                for n in TURN_BEHIND.get(c, ()):
                    turn_x(n)
                for n in PRODUCT_BEHIND.get(c, ()):
                    layer0_products(n)
            for g in range(GROUPS):
                ahead = g + LEAD if 1 <= g < GROUPS - LEAD else None
                first = 2 if g == 1 else 0
                if g >= 1:
                    open_sum(0, g - 1, range(first))
                if ahead:
                    layer0_products(2 * ahead)
                if g == FOLD_GROUP + 1:
                    sum_maxima()
                if g >= 1:
                    cuts = (TPG, TPG) if g < 3 else (2, TPG) if g == 3 else (1, 3)
                    open_sum(0, g - 1, range(first, cuts[0]))
                    if ahead:
                        layer0_products(2 * ahead + 1)
                    neighbour_sums(g, AHEAD * CT, JT)
                    open_sum(0, g - 1, range(*cuts))
                columns(g)
                if g == 0:
                    for half in range(2):
                        layer0_products(2 * LEAD + half)
                if g >= 1:
                    open_sum(0, g - 1, range(cuts[1], TPG))
                if g >= 2:
                    pe.wait_ge(S["comb_taken"], g + 1)
                dst = acc1 if g == 1 else work
                for j in range(TPG * g):
                    aggregate(dst, g, j, j == 0, False)
                if g == FOLD_GROUP:
                    fold_weights()
                if g + 1 < GROUPS:
                    neighbour_sums(g + 1, 0, AHEAD * CT)
                if g >= 1:
                    for k in range(TPG):
                        pe.wait_ge(S["lo_ready"], TPG * g + k + 1)
                        last = aggregate(dst, g, TPG * g + k, False, g > 1 and k == TPG - 1)
                    if g >= 2:
                        last.then_inc(S["sum_ready"], 1)
                        open_sum(1, g, range(TPG))
                    if g == FOLD_GROUP:
                        fold_bias()
            open_sum(0, GROUPS - 1, range(TPG))

            def turn_x1(n):
                for h in range(2):
                    bank = (psS if h == 0 else psX)[:, :].bitcast(F16)
                    if n >= 1:
                        pe.wait_ge(S["x1T_ready"], 2 * (n - 1) + h + 1)
                    elif h == 0:
                        pe.wait_ge(S["ident16_ready"], 1)
                        pe.wait_ge(S["srow_ready"], GROUPS)
                    for k in range(2):
                        for part in range(2):
                            for f in range(DH):
                                q = (2 * k + part) * DH + f
                                o = ((FINAL_ORDER[n] * TPG + 2 * h + k) * 2 + part) * D + f * P
                                last = nc.tensor.transpose(bank[:, q * P:(q + 1) * P], x1hl[:, o:o + P],
                                                           ident16[:, :])
                    last.then_inc(S["xt_ready"], 1)

            def layer1_products(n, k):
                t = n * TPG + k
                b = (t % 2) * 512
                g = FINAL_ORDER[n]
                if k == 0:
                    pe.wait_ge(S["agg_lo"], n + 1)
                if n == GROUPS - 1 and k == 2:
                    pe.wait_ge(S["agg_lo"], n + 2)
                if t == 0:
                    pe.wait_ge(S["bias_ready"], 1)
                    pe.wait_ge(S["wparts_ready"], 3)
                if t < 2:
                    pe.wait_ge(S["whole1_ready"], 1)
                else:
                    pe.wait_ge(S["v_ready"], t - 1)
                hi, lo = sum_parts(g, 0), sum_parts(g, 1)
                for h in range(DH):
                    o = h * IW + k * P
                    for m, (lhs, rhs) in enumerate(((hi, wnb_hi), (hi, wnb_lo), (lo, wnb_hi2))):
                        mm(fin[:, b:b + D], lhs[:, o:o + P], rhs[:, h * D:(h + 1) * D],
                           start=(h == 0 and m == 0), stop=(h == DH - 1 and m == 2))
                mm(fin[:, b + D:b + 2 * D], ones3[:, :], bias3[:, :], start=True, stop=False)
                if k % 2 == 0:
                    pe.wait_ge(S["x1T_ready"], 2 * n + k // 2 + 1)
                for h in range(DH):
                    for m, (part, rhs) in enumerate(((0, wself_hi), (0, wself_lo), (1, wself_hi))):
                        o = ((2 * k + part) * DH + h) * P
                        last = mm(fin[:, b + D:b + 2 * D], x1T[n % 2][:, o:o + P], rhs[:, h * D:(h + 1) * D],
                                  start=False, stop=(h == DH - 1 and m == 2))
                last.then_inc(S["fin_ready"], 1)

            def sum_rest(m, tiles):
                g = FINAL_ORDER[m]
                for j in tiles:
                    last = aggregate(work if m % 2 else acc0, g, j, j == TPG * (g + 1), j == JT - 1)
                    if j == JT - 1:
                        last.then_inc(S["sum2_ready"], 1)

            turn_x1(0)
            for n in range(GROUPS):
                todo = [(m, j) for m in SUM_STEPS if n in SUM_STEPS[m] for j in share(m, n)]
                if n == SUM_STEPS.get(todo[0][0], [None])[0] if todo else False:
                    m = todo[0][0]
                    pe.wait_ge(S["agg_ready"], m - 2 if m > 3 else 1)
                parts = LAST_GATHER if n == GROUPS - 2 else TPG
                for k in range(TPG):
                    if k == (3 if n == GROUPS - 2 else 2) and n + 1 < GROUPS:
                        turn_x1(n + 1)
                    for m, j in todo[len(todo) * k // parts:len(todo) * (k + 1) // parts]:
                        sum_rest(m, [j])
                    layer1_products(n, k)


FINAL_ORDER = [GROUPS - 1, 0, 1] + list(range(GROUPS - 2, 1, -1))
SUM_STEPS = {3: [0], 4: [1], 5: [2], 6: [3, 4], 7: [5, 6]}


def share(m, n):
    first = TPG * (FINAL_ORDER[m] + 1)
    steps = SUM_STEPS[m]
    i = steps.index(n)
    cut = [first + (JT - first) * q // len(steps) for q in range(len(steps) + 1)]
    return range(cut[i], cut[i + 1])


def kernel(**inputs):
    import numpy as _np
    import concourse.bacc as _bacc
    from concourse import mybir as _mybir
    from concourse.bass_utils import run_bass_kernel_spmd as _run

    a = {k: _np.asarray(v) for k, v in inputs.items()}
    x = a["x"]
    rows = lambda w, t: w.reshape(t, P, -1).transpose(1, 0, 2).reshape(P, -1)
    bias = _np.concatenate([a["L1_gnn_b_self"], a["L1_gnn_b_nb"]]).reshape(2 * DH, P)
    comb = _np.zeros((P, 2), _np.float32)
    for q in range(4):
        comb[q * SREP:q * SREP + 3, 0] = 1.0
        comb[q * SREP + 3, 1] = 1.0
    arrays = {
        "adjT": a["adj"].reshape(GROUPS, IW, CHUNKS, CT, P).transpose(0, 2, 4, 3, 1)
                        .reshape(GROUPS * CHUNKS, P, CT * IW),
        "xtile": x.reshape(GROUPS, TPG, P, D).transpose(0, 2, 1, 3).reshape(GROUPS, P, TPG * D),
        "xT": x.T.reshape(DH, P, GROUPS, IW).transpose(2, 1, 0, 3).reshape(GROUPS, P, DH * IW),
        "xcol": x[:, 0].reshape(JT, P).T,
        "w0T": rows(a["L0_gnn_w_self"].T, DH),
        "wnT": rows(a["L0_gnn_w_neigh"].T, DH),
        "wsT": rows(a["L1_gnn_W_self"].T, DH),
        "wbT": rows(a["L1_gnn_W_nb"].T, DH),
        "wc": rows(a["L1_gnn_W_comb"], 2 * DH),
        "bcol": _np.repeat(bias.T, 3, axis=1),
        "bcomb": _np.broadcast_to(a["L1_gnn_b_comb"], (3, D)),
        "ident": _np.eye(P, dtype=_np.float32),
        "comb": comb,
        "sel": _np.eye(3, dtype=_np.float32),
    }
    arrays = {k + "_dram": _np.ascontiguousarray(v) for k, v in arrays.items()}
    nc = _bacc.Bacc("TRN2", target_bir_lowering=False, num_devices=1)
    args = [nc.dram_tensor(k, v.shape, _mybir.dt.from_np(v.dtype), kind="ExternalInput").ap()
            for k, v in arrays.items()]
    out = nc.dram_tensor("out_dram", (GROUPS, P, TPG * D), F32, kind="ExternalOutput").ap()
    build(nc, *args, out)
    r = _run(nc, [arrays], core_ids=[0]).results[0]["out_dram"]
    return r.reshape(GROUPS, P, TPG, D).transpose(0, 2, 1, 3).reshape(N, D)
```
